# Optimizing a Trainium2 kernel written in Bass

```python
import numpy as np
import jax
import jax.numpy as jnp

def _softmax(x, axis=-1):
    return jax.nn.softmax(x, axis=axis)

def _gelu(x):
    return jax.nn.gelu(x, approximate=True)

def _silu(x):
    return jax.nn.silu(x)

def _sigmoid(x):
    return jax.nn.sigmoid(x)

def _layernorm(x, axis=-1, eps=1e-05):
    m = jnp.mean(x, axis=axis, keepdims=True)
    v = jnp.var(x, axis=axis, keepdims=True)
    return (x - m) / jnp.sqrt(v + eps)

def _scatter_add(tgt, idx, src, axis=0):
    return tgt.at[idx].add(src)

def _segment_sum(src, seg, n):
    return jax.ops.segment_sum(src, seg, n)
kernel_name = 'mk_seq_postln_d1_jaxref_r4_1df04d'

def setup_inputs(seed: int=0):
    np.random.seed(seed)
    _w = jnp.asarray

    def _L0_attn_setup():
        import math
        import jax, jax.numpy as jnp
        import numpy as np
        HIDDEN = 256
        NUM_LAYERS = 24
        LAYER_ID = 4

        def _time_params():
            h = HIDDEN
            ratio_0_to_1 = LAYER_ID / (NUM_LAYERS - 1)
            ratio_1_to_almost_0 = 1.0 - LAYER_ID / NUM_LAYERS
            zigzag = 0.5 * (jnp.arange(1, h + 1) % 3 - 1)
            time_first = jnp.full(h, math.log(0.3)) + zigzag
            idx = jnp.arange(0, h)
            time_decay = -5 + 8 * (idx / (h - 1)) ** (0.7 + 1.3 * ratio_0_to_1)
            x = jnp.arange(h) / h
            time_mix_key = jnp.power(x, ratio_1_to_almost_0)
            time_mix_value = time_mix_key + 0.3 * ratio_0_to_1
            time_mix_receptance = jnp.power(x, 0.5 * ratio_1_to_almost_0)
            return (time_decay.astype(jnp.float32), time_first.astype(jnp.float32), time_mix_key.astype(jnp.float32), time_mix_value.astype(jnp.float32), time_mix_receptance.astype(jnp.float32))

        def _wkv(time_decay, time_first, k, v):
            B, T, H = k.shape
            td = -jnp.exp(time_decay.astype(jnp.float32))
            tf = time_first.astype(jnp.float32)
            kT = jnp.swapaxes(k, 0, 1).astype(jnp.float32)
            vT = jnp.swapaxes(v, 0, 1).astype(jnp.float32)

            def step(carry, kv):
                num, den, mx = carry
                ck, cv = kv
                max_out = jnp.maximum(mx, ck + tf)
                e1 = jnp.exp(mx - max_out)
                e2 = jnp.exp(ck + tf - max_out)
                out = (e1 * num + e2 * cv) / (e1 * den + e2)
                max_st = jnp.maximum(mx + td, ck)
                e1s = jnp.exp(mx + td - max_st)
                e2s = jnp.exp(ck - max_st)
                return ((e1s * num + e2s * cv, e1s * den + e2s, max_st), out)
            init = (jnp.zeros((B, H), jnp.float32), jnp.zeros((B, H), jnp.float32), jnp.full((B, H), -1e+38, jnp.float32))
            _, outT = jax.lax.scan(step, init, (kT, vT))
            return jnp.swapaxes(outT, 0, 1).astype(k.dtype)
        key = jax.random.key(seed)
        k0, k1, k2, k3, k4 = jax.random.split(key, 5)
        B, T, H = (4, 1024, HIDDEN)
        td, tf, tmk, tmv, tmr = _time_params()
        scale = 0.02
        return {'hidden': jax.random.normal(k0, (B, T, H), dtype=jnp.float32), 'Wk': jax.random.normal(k1, (H, H), dtype=jnp.float32) * scale, 'Wv': jax.random.normal(k2, (H, H), dtype=jnp.float32) * scale, 'Wr': jax.random.normal(k3, (H, H), dtype=jnp.float32) * scale, 'Wo': jax.random.normal(k4, (H, H), dtype=jnp.float32) * scale, 'time_decay': td, 'time_first': tf, 'time_mix_key': tmk, 'time_mix_value': tmv, 'time_mix_receptance': tmr}
    _L0_attn_in = _L0_attn_setup()

    def _L0_ffn_setup():
        import jax, jax.numpy as jnp
        import numpy as np
        LN_EPS = 1e-05

        def layer_norm(x, g, b):
            mu = jnp.mean(x, axis=-1, keepdims=True)
            var = jnp.mean(jnp.square(x - mu), axis=-1, keepdims=True)
            return (x - mu) * jax.lax.rsqrt(var + LN_EPS) * g + b

        def ternary_quant(w):
            scale = 1.0 / jnp.clip(jnp.mean(jnp.abs(w)), 1e-05)
            wq = jnp.clip(jnp.round(w * scale), -1.0, 1.0) / scale
            return w + jax.lax.stop_gradient(wq - w)
        key = jax.random.key(seed)
        ks = jax.random.split(key, 3)
        dim, hidden = (256, 1024)
        B, S = (8, 256)
        x = jax.random.normal(ks[0], (B, S, dim), dtype=jnp.float32)
        w1 = jax.random.normal(ks[1], (hidden, dim), dtype=jnp.float32) * 0.02
        w2 = jax.random.normal(ks[2], (dim, hidden), dtype=jnp.float32) * 0.02
        return {'x': x, 'ln1_g': jnp.ones((dim,), jnp.float32), 'ln1_b': jnp.zeros((dim,), jnp.float32), 'w1': w1, 'b1': jnp.zeros((hidden,), jnp.float32), 'ln2_g': jnp.ones((hidden,), jnp.float32), 'ln2_b': jnp.zeros((hidden,), jnp.float32), 'w2': w2, 'b2': jnp.zeros((dim,), jnp.float32)}
    _L0_ffn_in = _L0_ffn_setup()
    _d = {'L0_attn_hidden': _L0_attn_in['hidden'], 'L0_attn_Wk': _L0_attn_in['Wk'], 'L0_attn_Wv': _L0_attn_in['Wv'], 'L0_attn_Wr': _L0_attn_in['Wr'], 'L0_attn_Wo': _L0_attn_in['Wo'], 'L0_attn_time_decay': _L0_attn_in['time_decay'], 'L0_attn_time_first': _L0_attn_in['time_first'], 'L0_attn_time_mix_key': _L0_attn_in['time_mix_key'], 'L0_attn_time_mix_value': _L0_attn_in['time_mix_value'], 'L0_attn_time_mix_receptance': _L0_attn_in['time_mix_receptance'], 'L0_ffn_ln1_g': _L0_ffn_in['ln1_g'], 'L0_ffn_ln1_b': _L0_ffn_in['ln1_b'], 'L0_ffn_w1': _L0_ffn_in['w1'], 'L0_ffn_b1': _L0_ffn_in['b1'], 'L0_ffn_ln2_g': _L0_ffn_in['ln2_g'], 'L0_ffn_ln2_b': _L0_ffn_in['ln2_b'], 'L0_ffn_w2': _L0_ffn_in['w2'], 'L0_ffn_b2': _L0_ffn_in['b2']}
    _x0 = _d['L0_attn_hidden']
    _d['L0_attn_hidden'] = jax.random.normal(jax.random.fold_in(jax.random.key(seed), 1), (8, 2048, 256), dtype=_x0.dtype)
    del _x0
    return _d

def reference(L0_attn_hidden, L0_attn_Wk, L0_attn_Wv, L0_attn_Wr, L0_attn_Wo, L0_attn_time_decay, L0_attn_time_first, L0_attn_time_mix_key, L0_attn_time_mix_value, L0_attn_time_mix_receptance, L0_ffn_ln1_g, L0_ffn_ln1_b, L0_ffn_w1, L0_ffn_b1, L0_ffn_ln2_g, L0_ffn_ln2_b, L0_ffn_w2, L0_ffn_b2):

    def _L0_attn_ref(hidden, Wk, Wv, Wr, Wo, time_decay, time_first, time_mix_key, time_mix_value, time_mix_receptance):
        import math
        import jax, jax.numpy as jnp
        import numpy as np
        HIDDEN = 256
        NUM_LAYERS = 24
        LAYER_ID = 4

        def _time_params():
            h = HIDDEN
            ratio_0_to_1 = LAYER_ID / (NUM_LAYERS - 1)
            ratio_1_to_almost_0 = 1.0 - LAYER_ID / NUM_LAYERS
            zigzag = 0.5 * (jnp.arange(1, h + 1) % 3 - 1)
            time_first = jnp.full(h, math.log(0.3)) + zigzag
            idx = jnp.arange(0, h)
            time_decay = -5 + 8 * (idx / (h - 1)) ** (0.7 + 1.3 * ratio_0_to_1)
            x = jnp.arange(h) / h
            time_mix_key = jnp.power(x, ratio_1_to_almost_0)
            time_mix_value = time_mix_key + 0.3 * ratio_0_to_1
            time_mix_receptance = jnp.power(x, 0.5 * ratio_1_to_almost_0)
            return (time_decay.astype(jnp.float32), time_first.astype(jnp.float32), time_mix_key.astype(jnp.float32), time_mix_value.astype(jnp.float32), time_mix_receptance.astype(jnp.float32))

        def _wkv(time_decay, time_first, k, v):
            B, T, H = k.shape
            td = -jnp.exp(time_decay.astype(jnp.float32))
            tf = time_first.astype(jnp.float32)
            kT = jnp.swapaxes(k, 0, 1).astype(jnp.float32)
            vT = jnp.swapaxes(v, 0, 1).astype(jnp.float32)

            def step(carry, kv):
                num, den, mx = carry
                ck, cv = kv
                max_out = jnp.maximum(mx, ck + tf)
                e1 = jnp.exp(mx - max_out)
                e2 = jnp.exp(ck + tf - max_out)
                out = (e1 * num + e2 * cv) / (e1 * den + e2)
                max_st = jnp.maximum(mx + td, ck)
                e1s = jnp.exp(mx + td - max_st)
                e2s = jnp.exp(ck - max_st)
                return ((e1s * num + e2s * cv, e1s * den + e2s, max_st), out)
            init = (jnp.zeros((B, H), jnp.float32), jnp.zeros((B, H), jnp.float32), jnp.full((B, H), -1e+38, jnp.float32))
            _, outT = jax.lax.scan(step, init, (kT, vT))
            return jnp.swapaxes(outT, 0, 1).astype(k.dtype)
        shifted = jnp.pad(hidden, ((0, 0), (1, 0), (0, 0)))[:, :-1]
        k_in = hidden * time_mix_key + shifted * (1 - time_mix_key)
        v_in = hidden * time_mix_value + shifted * (1 - time_mix_value)
        r_in = hidden * time_mix_receptance + shifted * (1 - time_mix_receptance)
        k = k_in @ Wk
        v = v_in @ Wv
        r = jax.nn.sigmoid(r_in @ Wr)
        rwkv = _wkv(time_decay, time_first, k, v)
        return r * rwkv @ Wo

    def _L0_ffn_ref(x, ln1_g, ln1_b, w1, b1, ln2_g, ln2_b, w2, b2):
        import jax, jax.numpy as jnp
        import numpy as np
        LN_EPS = 1e-05

        def layer_norm(x, g, b):
            mu = jnp.mean(x, axis=-1, keepdims=True)
            var = jnp.mean(jnp.square(x - mu), axis=-1, keepdims=True)
            return (x - mu) * jax.lax.rsqrt(var + LN_EPS) * g + b

        def ternary_quant(w):
            scale = 1.0 / jnp.clip(jnp.mean(jnp.abs(w)), 1e-05)
            wq = jnp.clip(jnp.round(w * scale), -1.0, 1.0) / scale
            return w + jax.lax.stop_gradient(wq - w)
        h = layer_norm(x, ln1_g, ln1_b)
        h = jnp.einsum('bsd,hd->bsh', h, ternary_quant(w1)) + b1
        h = jax.nn.gelu(h, approximate=False)
        h = layer_norm(h, ln2_g, ln2_b)
        out = jnp.einsum('bsh,dh->bsd', h, ternary_quant(w2)) + b2
        return out
    x = L0_attn_hidden
    x = _layernorm(x + _L0_attn_ref(x, L0_attn_Wk, L0_attn_Wv, L0_attn_Wr, L0_attn_Wo, L0_attn_time_decay, L0_attn_time_first, L0_attn_time_mix_key, L0_attn_time_mix_value, L0_attn_time_mix_receptance), axis=-1)
    x = _layernorm(x + _L0_ffn_ref(x, L0_ffn_ln1_g, L0_ffn_ln1_b, L0_ffn_w1, L0_ffn_b1, L0_ffn_ln2_g, L0_ffn_ln2_b, L0_ffn_w2, L0_ffn_b2), axis=-1)
    return x

_drawn_inputs = setup_inputs


def setup_inputs(seed=0):
    import zlib

    import numpy as np

    out = dict(_drawn_inputs(seed))
    spreads = {'L0_ffn_ln1_g': (1.0, 0.2),
     'L0_ffn_ln1_b': (0.0, 0.1),
     'L0_ffn_b1': (0.0, 0.1),
     'L0_ffn_ln2_g': (1.0, 0.2),
     'L0_ffn_ln2_b': (0.0, 0.1),
     'L0_ffn_b2': (0.0, 0.1)}
    factors = {'L0_attn_Wk': 8.0,
     'L0_attn_Wr': 8.0,
     'L0_attn_time_decay': 3.1,
     'L0_attn_time_first': 8.0,
     'L0_attn_time_mix_key': 8.0,
     'L0_attn_time_mix_value': 5.927,
     'L0_attn_time_mix_receptance': 8.0}
    for name, (base, spread) in spreads.items():
        noise = np.random.default_rng([zlib.crc32(name.encode()), seed]).standard_normal(out[name].shape)
        drawn = base * np.exp(spread * noise) if base else spread * noise
        out[name] = jnp.asarray(drawn.astype(out[name].dtype))
    for name, factor in factors.items():
        out[name] = (out[name] * factor).astype(out[name].dtype)
    return out
```

```python
from contextlib import ExitStack

import numpy as np

import concourse.bass as bass
from concourse import mybir

F32 = mybir.dt.float32
ALU = mybir.AluOpType
ACT = mybir.ActivationFunctionType
AX = mybir.AxisListType

P = 128
TOK = 512
Q = TOK // P
EPS = 1e-5
NO_MAX = -1e38


def build(nc, x_in, x_by_channel, Wk, Wv, Wr, Wo, time_decay, time_first, mix_k, mix_v, mix_r,
          ln1_g, ln1_b, w1, b1, ln2_g, ln2_b, w2, b2, out):
    B, T, H = x_in.shape
    F = w1.shape[1]
    KC = H // P
    FC = F // P
    JT = T // TOK
    NT = B * JT
    assert H == KC * P and KC == 2 and F == FC * P and T == JT * TOK and Q == 4 and JT == 4

    x_rows = x_in.rearrange("b (j q p) h -> (b j) p q h", q=Q, p=P)
    x_cols = x_by_channel.rearrange("b (c p) t -> p b c t", p=P)
    out_rows = out.rearrange("b (j q p) h -> (b j) p q h", q=Q, p=P)

    with ExitStack() as ctx:
        def sb(name, shape):
            return ctx.enter_context(nc.sbuf_tensor(name, shape, F32))

        def ps(name, shape):
            return ctx.enter_context(nc.psum_tensor(name, shape, F32))

        def sem(name):
            return ctx.enter_context(nc.semaphore(name))

        ident = sb("ident", [P, P])
        ones = sb("ones", [P, P])
        wkvr = sb("wkvr", [P, 3, KC, H])
        wo = sb("wo", [P, KC, H])
        w1T = sb("w1T", [P, KC, F])
        w2c = sb("w2c", [P, FC, H + 1])
        tcol = sb("tcol", [P, 5, KC])
        ntd = sb("ntd", [P, KC])
        td = sb("td", [P, KC])
        htf = sb("htf", [P, KC])
        omix = sb("omix", [P, 3, KC])
        lncol = sb("lncol", [P, 2, KC])
        fcol = sb("fcol", [P, 3, FC])
        wabs = sb("wabs", [P, 2])
        wmean = sb("wmean", [P, 2])
        wscale = sb("wscale", [P, 2])
        const_row = sb("const_row", [P, H])
        half_rows = sb("half_rows", [P, H])
        init = sb("init", [P, 4])
        nhalf = sb("nhalf", [P, Q])

        x_tok = sb("x_tok", [P, 4, Q, H])
        xT = sb("xT", [P, JT, KC, TOK + 1])
        keep = sb("keep", [P, 2, TOK])
        mixed = sb("mixed", [P, 3, KC, TOK])
        hist = sb("hist", [P, KC, 4, TOK + 1])
        dlt = sb("dlt", [P, KC, TOK])
        e1 = sb("e1", [P, KC, TOK])
        e2 = sb("e2", [P, KC, TOK])
        m2 = sb("m2", [P, KC, TOK])
        beta = sb("beta", [P, KC, TOK])
        obeta = sb("obeta", [P, KC, TOK])
        bv = sb("bv", [P, KC, TOK])
        wdf = sb("wdf", [P, KC, TOK])
        tr = sb("tr", [P, KC, TOK])
        rwkv = sb("rwkv", [P, KC, TOK])
        y_tok = sb("y_tok", [P, Q, H])
        hn = sb("hn", [P, Q, H])
        x1c = sb("x1c", [P, 4, Q, H])
        hT = sb("hT", [P, KC, TOK])
        u = sb("u", [P, FC, TOK])
        usq = sb("usq", [P, FC, TOK])
        proj = sb("proj", [P, Q, H + 2])
        z_tok = sb("z_tok", [P, Q, H])
        bn1 = sb("bn1", [P, Q, 6])
        mv1 = sb("mv1", [P, Q, 2])
        rs1 = sb("rs1", [P, 6, Q])
        rs2 = sb("rs2", [P, 8, Q])
        bn3 = sb("bn3", [P, Q, 6])
        mv3 = sb("mv3", [P, Q, 2])
        rs3 = sb("rs3", [P, 2, Q])

        turn_ps = ps("turn_ps", [P, 512])
        kvr_ps = ps("kvr_ps", [P, 3, 512])
        up_ps = ps("up_ps", [P, 2, 512])
        row_ps = ps("row_ps", [P, 2, 512])

        ld_w = sem("ld_w"); ld_xT = [sem(f"ld_xT{b}") for b in range(4)]; ld_x = [sem(f"ld_x{b}") for b in range(4)]
        st_out = sem("st_out")
        s_passed = sem("s_passed"); s_const = sem("s_const"); s_ident = sem("s_ident")
        w_cols = sem("w_cols"); w_col2 = sem("w_col2")
        w_abs = sem("w_abs"); w_sum = sem("w_sum"); w_scl = sem("w_scl"); w_tern = sem("w_tern")
        w_bias = sem("w_bias")
        w_rows = sem("w_rows"); w_rowc = sem("w_rowc"); w_done = sem("w_done")
        xt_first = sem("xt_first")
        kept = sem("kept"); mix_done = sem("mix_done")
        kvr_ready = sem("kvr_ready"); carried = sem("carried")
        mx_done = sem("mx_done"); dlt_done = sem("dlt_done")
        m_done = sem("m_done"); e_done = sem("e_done"); den_done = sem("den_done")
        ln_done = sem("ln_done"); barg_done = sem("barg_done"); garg_done = sem("garg_done")
        beta_done = sem("beta_done"); obeta_done = sem("obeta_done"); bv_done = sem("bv_done")
        avg_done = sem("avg_done"); wdf_done = sem("wdf_done"); gam_done = sem("gam_done")
        tr_done = sem("tr_done"); g1_done = sem("g1_done"); o1_done = sem("o1_done")
        rwkv_done = sem("rwkv_done")
        att_ready = sem("att_ready"); y_done = sem("y_done"); bn1_done = sem("bn1_done")
        mv1_done = sem("mv1_done"); rs1_step = sem("rs1_step"); rs1_fine = sem("rs1_fine"); rs1_done = sem("rs1_done")
        x1_done = sem("x1_done"); hn_done = sem("hn_done"); x1c_done = sem("x1c_done")
        ht_ready = sem("ht_ready"); ht_evac = sem("ht_evac")
        up_ready = sem("up_ready"); u_done = sem("u_done"); usq_done = sem("usq_done")
        down_ready = sem("down_ready"); proj_done = sem("proj_done")
        rs2_step = sem("rs2_step"); rs2_done = sem("rs2_done")
        z_done = sem("z_done"); bn3_done = sem("bn3_done"); mv3_done = sem("mv3_done")
        rs3_step = sem("rs3_step"); rs3_done = sem("rs3_done"); fin_done = sem("fin_done")

        w1_raw = u[:].rearrange("p c t -> p (c t)")[:, 0:FC * H].rearrange("p (c f) -> p c f", c=KC)
        w2_raw = u[:].rearrange("p c t -> p (c t)")[:, FC * H:2 * FC * H].rearrange("p (c h) -> p c h", c=FC)
        tern_neg = usq[:].rearrange("p c t -> p (c t)")[:, 0:FC * H]
        wabs_out = usq[:].rearrange("p c t -> p (c t)")
        w2_tern = x1c[:].rearrange("p b q h -> p (b q) h")[:, 0:FC, :]
        bias_rows = x1c[:].rearrange("p b q h -> p (b q h)")[:, FC * H:FC * H + FC * P].rearrange("p (c m) -> p c m", c=FC)
        b2_row = z_tok[:, 0, :]

        block = ctx.enter_context(nc.Block())

        def settled(eng):
            eng.sem_inc(s_passed, 1)

        @block.sync
        def _(sp):
            def load(i, j, b):
                sp.dma_start(x_tok[:, j], x_rows[i]).then_inc(ld_x[j], 16)
                for c in range(KC):
                    if j == 0:
                        sp.dma_start(xT[:, 0, c, 1:TOK + 1], x_cols[:, b, c, 0:TOK]).then_inc(ld_xT[0], 16)
                    else:
                        sp.dma_start(xT[:, j, c, :], x_cols[:, b, c, j * TOK - 1:(j + 1) * TOK]).then_inc(ld_xT[j], 16)

            load(0, 0, 0)
            for n, v in enumerate((time_decay, time_first, mix_k, mix_v, mix_r)):
                sp.dma_start(tcol[:, n, :], v).then_inc(ld_w, 16)
            for n, v in enumerate((ln1_g, ln1_b)):
                sp.dma_start(lncol[:, n, :], v).then_inc(ld_w, 16)
            for n, v in enumerate((b1, ln2_g, ln2_b)):
                sp.dma_start(fcol[:, n, :], v).then_inc(ld_w, 16)
            for n, w in enumerate((Wk, Wv, Wr)):
                sp.dma_start(wkvr[:, n], w.rearrange("(c p) n -> p c n", p=P)).then_inc(ld_w, 16)
            sp.wait_ge(s_const, 1)
            sp.dma_start(b2_row[0:1, :], b2.rearrange("(a n) -> a n", a=1)).then_inc(ld_w, 16)
            sp.dma_start(w1_raw, w1.rearrange("(c p) n -> p c n", p=P)).then_inc(w_cols, 16)
            sp.dma_start(w2_raw, w2.rearrange("(c p) n -> p c n", p=P)).then_inc(w_cols, 16)
            sp.dma_start(wo[:], Wo.rearrange("(c p) n -> p c n", p=P)).then_inc(w_cols, 16)
            for j in range(1, JT):
                load(j, j, 0)

            def tile(i, j, b, has_load, has_fin):
                if has_load:
                    sp.wait_ge(y_done, i)
                    settled(sp)
                    sp.wait_ge(mix_done, 6 * i)
                    settled(sp)
                    load(i + 3, (j + 3) % JT, b if j == 0 else b + 1)
                if has_fin:
                    sp.wait_ge(fin_done, i - 1)
                    settled(sp)
                    sp.dma_start(out_rows[i - 2], z_tok[:]).then_inc(st_out, 16)

            for i in range(1, JT):
                tile(i, i, 0, True, i >= 2)
            with sp.Fori(1, B - 1) as b:
                for j in range(JT):
                    tile(b * JT + j, j, b, True, True)
            for i in range(NT - JT, NT + 2):
                tile(i, i % JT, i // JT, i + 3 < NT, True)
            sp.wait_ge(st_out, 16 * NT)

        @block.tensor
        def _(pe):
            def turn_h(i):
                pe.wait_ge(hn_done, i + 1)
                for c in range(KC):
                    if not (isinstance(i, int) and i == 0 and c == 0):
                        pe.wait_ge(ht_evac, KC * i + c)
                    for q in range(Q):
                        m = pe.transpose(turn_ps[:, q * P:(q + 1) * P],
                                         hn[:, q, c * P:(c + 1) * P], ident[:])
                    m.then_inc(ht_ready, 1)

            def kvr(i, h, first=False):
                n = KC * i + h
                pe.wait_ge(mix_done, 6 * (i + 1))
                for w, used in ((0, dlt_done), (1, wdf_done), (2, tr_done)):
                    if not (first and h == 0):
                        pe.wait_ge(used, n)
                    for c in range(KC):
                        m = pe.matmul(kvr_ps[:, w, :], wkvr[:, w, c, h * P:(h + 1) * P],
                                      mixed[:, w, c, :], start=(c == 0), stop=(c == KC - 1))
                    m.then_inc(kvr_ready, 1)

            def up(i, c0, c1, first=False):
                pe.wait_ge(ht_evac, KC * (i + 1))
                for f in range(c0, c1):
                    if not (first and f < 2):
                        pe.wait_ge(u_done, FC * i + f - 1)
                    for c in range(KC):
                        m = pe.matmul(up_ps[:, f % 2, :], w1T[:, c, f * P:(f + 1) * P],
                                      hT[:, c, :], start=(c == 0), stop=(c == KC - 1))
                    m.then_inc(up_ready, 1)

            def down(i, first=False):
                pe.wait_ge(usq_done, FC * (i + 1))
                for q in range(Q):
                    if q < 2:
                        pe.wait_ge(y_done, i + 1)
                    else:
                        pe.wait_ge(proj_done, Q * i + q - 1)
                    t = slice(q * P, (q + 1) * P)
                    for f in range(FC):
                        pe.matmul(row_ps[:, q % 2, 0:H + 1], u[:, f, t], w2c[:, f, :],
                                  start=(f == 0), stop=(f == FC - 1))
                    for f in range(FC):
                        m = pe.matmul(row_ps[:, q % 2, H + 1:H + 2], usq[:, f, t], ones[:, 0:1],
                                      start=(f == 0), stop=(f == FC - 1))
                    m.then_inc(down_ready, 1)

            def att(i, first=False):
                pe.wait_ge(rwkv_done, KC * (i + 1))
                if not first:
                    pe.wait_ge(proj_done, Q * i)
                for g in range(2):
                    for q in range(2):
                        t = slice((2 * g + q) * P, (2 * g + q + 1) * P)
                        for c in range(KC):
                            m = pe.matmul(row_ps[:, g, q * H:(q + 1) * H], rwkv[:, c, t], wo[:, c, :],
                                          start=(c == 0), stop=(c == KC - 1))
                m.then_inc(att_ready, 1)

            pe.wait_ge(s_ident, 2)
            pe.wait_ge(s_const, 3)
            pe.wait_ge(w_abs, 2)
            pe.matmul(row_ps[:, 0, 0:2], ones[:], wabs[:], start=True, stop=True).then_inc(w_sum, 1)
            pe.wait_ge(w_bias, 1)
            pe.wait_ge(w_tern, 3)
            pe.wait_ge(ld_w, 16 * 14)
            pe.wait_ge(w_scl, 2)
            for f in range(FC):
                pe.matmul(row_ps[:, 0, 0:H], bias_rows[:, f, :], w2_tern[:, f, :],
                          start=(f == 0), stop=(f == FC - 1))
            for f in range(FC):
                pe.matmul(row_ps[:, 1, 0:H], ones[:], w2c[:, f, 0:H],
                          start=(f == 0), stop=(f == FC - 1))
            pe.matmul(row_ps[:, 1, H:2 * H], ones[:], b2_row, start=True, stop=True).then_inc(w_rows, 1)

            def step(i, j, first=False, has_next=True):
                kvr(i, 0, first=first)
                if not first:
                    turn_h(i - 1)
                    up(i - 1, 0, FC // 2, first=(isinstance(i, int) and i == 1))
                kvr(i, 1, first=first)
                if not first:
                    up(i - 1, FC // 2, FC)
                if not first:
                    down(i - 1)
                else:
                    pe.wait_ge(w_done, 1)
                att(i, first=first)

            step(0, 0, first=True)
            for i in range(1, JT):
                step(i, i)
            with pe.Fori(1, B - 1) as b:
                for j in range(JT):
                    step(b * JT + j, j)
            for i in range(NT - JT, NT):
                step(i, i % JT, has_next=i + 1 < NT)
            turn_h(NT - 1)
            up(NT - 1, 0, FC)
            down(NT - 1)

        @block.scalar
        def _(act):
            def evac_h(i, first=False):
                if not first:
                    act.wait_ge(up_ready, FC * i)
                for c in range(KC):
                    act.wait_ge(ht_ready, KC * i + c + 1)
                    act.activation(hT[:, c, :], turn_ps[:], ACT.Identity, bias=lncol[:, 1, c:c + 1],
                                   scale=lncol[:, 0, c:c + 1]).then_inc(ht_evac, 1)

            def gelus(i, c0, c1, first=False):
                if c0 == 0 and not first:
                    act.wait_ge(down_ready, Q * i)
                for f in range(c0, c1):
                    act.wait_ge(up_ready, FC * i + f + 1)
                    act.activation(u[:, f, :], up_ps[:, f % 2, :], ACT.Gelu, bias=fcol[:, 0, f:f + 1],
                                   scale=wmean[:, 0:1]).then_inc(u_done, 1)
                for f in range(c0, c1):
                    act.wait_ge(u_done, FC * i + f + 1)
                    act.activation(usq[:, f, :], u[:, f, :], ACT.Square).then_inc(usq_done, 1)

            def wkv(i, h):
                n = KC * i + h
                act.wait_ge(kvr_ready, 3 * n + 3)
                act.activation(tr[:, h, :], kvr_ps[:, 2, :], ACT.Tanh, scale=0.5).then_inc(tr_done, 1)
                act.wait_ge(m_done, 2 * n + 1)
                act.activation(e1[:, h, :], e1[:, h, :], ACT.Exp, bias=td[:, h:h + 1], scale=-1.0).then_inc(e_done, 1)
                act.wait_ge(m_done, 2 * n + 2)
                act.activation(e2[:, h, :], m2[:, h, :], ACT.Exp, bias=ntd[:, h:h + 1]).then_inc(e_done, 1)
                act.wait_ge(den_done, n + 1)
                act.activation(hist[:, h, 1, 1:TOK + 1], hist[:, h, 3, 1:TOK + 1], ACT.Ln).then_inc(ln_done, 1)
                act.wait_ge(barg_done, n + 1)
                act.activation(beta[:, h, :], beta[:, h, :], ACT.Exp, bias=ntd[:, h:h + 1]).then_inc(beta_done, 1)
                act.wait_ge(garg_done, n + 1)
                act.activation(dlt[:, h, :], dlt[:, h, :], ACT.Tanh, bias=htf[:, h:h + 1], scale=0.5).then_inc(gam_done, 1)

            def copy_down(i, first=False):
                if not first:
                    act.wait_ge(z_done, Q * i)
                for q in range(Q):
                    act.wait_ge(down_ready, Q * i + q + 1)
                    act.activation(proj[:, q, :], row_ps[:, q % 2, 0:H + 2], ACT.Copy).then_inc(proj_done, 1)

            act.wait_ge(ld_w, 16 * 14)
            act.activation(ntd[:], tcol[:, 0, :], ACT.Exp).then_inc(w_col2, 1)
            act.wait_ge(w_cols, 16 * 3)
            act.activation(wabs_out[:, 0:FC * H].rearrange("p (c f) -> p c f", c=KC), w1_raw, ACT.Abs, accum_out=wabs[:, 0:1]).then_inc(w_abs, 1)
            act.activation(wabs_out[:, FC * H:2 * FC * H].rearrange("p (c h) -> p c h", c=FC), w2_raw, ACT.Abs, accum_out=wabs[:, 1:2]).then_inc(w_abs, 1)

            def step(i, j, first=False, has_next=True):
                second = isinstance(i, int) and i == 1
                wkv(i, 0)
                if not first:
                    evac_h(i - 1, first=second)
                    gelus(i - 1, 0, FC // 2, first=second)
                wkv(i, 1)
                if not first:
                    gelus(i - 1, FC // 2, FC)
                if not first:
                    copy_down(i - 1, first=second)

            act.wait_ge(w_done, 1)
            step(0, 0, first=True)
            for i in range(1, JT):
                step(i, i)
            with act.Fori(1, B - 1) as b:
                for j in range(JT):
                    step(b * JT + j, j)
            for i in range(NT - JT, NT):
                step(i, i % JT, has_next=i + 1 < NT)
            evac_h(NT - 1)
            gelus(NT - 1, 0, FC)
            copy_down(NT - 1)

        @block.vector
        def _(v):
            def mix(i, j):
                for n in range(6):
                    w, c = n // KC, n % KC
                    v.wait_ge(kept, 6 * i + n + 1)
                    v.scalar_tensor_tensor(out=mixed[:, w, c, :], in0=xT[:, j % JT, c, 1:TOK + 1],
                                           scalar=tcol[:, 2 + w, c:c + 1], in1=keep[:, n % 2, :],
                                           op0=ALU.mult, op1=ALU.add).then_inc(mix_done, 1)

            def wkv_a(i, h):
                n = KC * i + h
                v.wait_ge(kvr_ready, 3 * n + 1)
                v.wait_ge(carried, n + 1)
                k = kvr_ps[:, 0, :]
                v.tensor_tensor_scan(hist[:, h, 0, 1:TOK + 1], td[:, h:h + 1].broadcast_to([P, TOK]), k,
                                     hist[:, h, 0, 0:1], ALU.add, ALU.max).then_inc(mx_done, 1)
                v.wait_ge(mx_done, n + 1)
                v.tensor_tensor(dlt[:, h, :], k, hist[:, h, 0, 0:TOK], ALU.subtract).then_inc(dlt_done, 1)

            def wkv_b(i, h):
                n = KC * i + h
                v.wait_ge(e_done, 2 * n + 2)
                v.tensor_tensor_scan(hist[:, h, 3, 1:TOK + 1], e1[:, h, :], e2[:, h, :],
                                     hist[:, h, 3, 0:1], ALU.mult, ALU.add).then_inc(den_done, 1)

            def wkv_c(i, h):
                n = KC * i + h
                val = kvr_ps[:, 1, :]
                v.wait_ge(kvr_ready, 3 * n + 2)
                v.wait_ge(beta_done, n + 1)
                v.tensor_tensor(bv[:, h, :], val, beta[:, h, :], ALU.mult).then_inc(bv_done, 1)
                v.wait_ge(bv_done, n + 1)
                v.wait_ge(obeta_done, n + 1)
                v.tensor_tensor_scan(hist[:, h, 2, 1:TOK + 1], obeta[:, h, :], bv[:, h, :],
                                     hist[:, h, 2, 0:1], ALU.mult, ALU.add).then_inc(avg_done, 1)
                v.wait_ge(avg_done, n + 1)
                v.tensor_tensor(wdf[:, h, :], val, hist[:, h, 2, 0:TOK], ALU.subtract).then_inc(wdf_done, 1)
                v.wait_ge(wdf_done, n + 1)
                v.wait_ge(gam_done, n + 1)
                v.scalar_tensor_tensor(out=wdf[:, h, :], in0=dlt[:, h, :], scalar=1.0, in1=wdf[:, h, :],
                                       op0=ALU.add, op1=ALU.mult).then_inc(g1_done, 1)
                v.wait_ge(g1_done, n + 1)
                v.scalar_tensor_tensor(out=wdf[:, h, :], in0=wdf[:, h, :], scalar=0.5, in1=hist[:, h, 2, 0:TOK],
                                       op0=ALU.mult, op1=ALU.add).then_inc(o1_done, 1)
                v.wait_ge(o1_done, n + 1)
                v.wait_ge(tr_done, n + 1)
                if h == 0:
                    v.wait_ge(att_ready, i)
                v.scalar_tensor_tensor(out=rwkv[:, h, :], in0=tr[:, h, :], scalar=1.0, in1=wdf[:, h, :],
                                       op0=ALU.add, op1=ALU.mult).then_inc(rwkv_done, 1)

            def z_part(i, j, first=False):
                if not first:
                    v.wait_ge(st_out, 16 * i)
                v.wait_ge(rs2_done, i + 1)
                v.wait_ge(x1c_done, i + 1)
                for q in range(Q):
                    v.scalar_tensor_tensor(out=z_tok[:, q, :], in0=proj[:, q, 0:H], scalar=rs2[:, 6, q:q + 1],
                                           in1=x1c[:, j % 4, q, :], op0=ALU.mult, op1=ALU.add).then_inc(z_done, 1)
                for q in range(Q):
                    v.wait_ge(z_done, Q * i + q + 1)
                    v.bn_stats(bn3[:, q, :], z_tok[:, q, :]).then_inc(bn3_done, 1)
                for q in range(Q):
                    v.wait_ge(bn3_done, Q * i + q + 1)
                    settled(v)
                    m = v.bn_aggr(mv3[:, q, :], bn3[:, q, :])
                m.then_inc(mv3_done, 1)

            def z_end(i):
                v.wait_ge(mv3_done, i + 1)
                v.wait_ge(rs3_done, i + 1)
                for q in range(Q):
                    m = v.tensor_scalar(z_tok[:, q, :], z_tok[:, q, :], mv3[:, q, 0:1], rs3[:, 1, q:q + 1],
                                        ALU.subtract, ALU.mult)
                m.then_inc(fin_done, 1)

            def ln1(i, j):
                v.wait_ge(att_ready, i + 1)
                v.wait_ge(ld_x[j], (i - j) // JT * 16 + 16 if isinstance(i, int) else (i - j) * 4 + 16)
                xq = x_tok[:, j % 4].rearrange("p (g q) h -> p g (q h)", g=2)
                yq = y_tok[:].rearrange("p (g q) h -> p g (q h)", g=2)
                for g in range(2):
                    m = v.tensor_tensor(yq[:, g], row_ps[:, g, :], xq[:, g], ALU.add)
                m.then_inc(y_done, 1)
                v.wait_ge(y_done, i + 1)
                for q in range(Q):
                    m = v.bn_stats(bn1[:, q, :], y_tok[:, q, :])
                m.then_inc(bn1_done, 1)
                v.wait_ge(bn1_done, i + 1)
                settled(v)
                for q in range(Q):
                    m = v.bn_aggr(mv1[:, q, :], bn1[:, q, :])
                m.then_inc(mv1_done, 1)
                v.wait_ge(mv1_done, i + 1)
                v.wait_ge(rs1_done, i + 1)
                for q in range(Q):
                    m = v.tensor_scalar(hn[:, q, :], y_tok[:, q, :], mv1[:, q, 0:1], rs1[:, 5, q:q + 1],
                                        ALU.subtract, ALU.mult)
                m.then_inc(hn_done, 1)
                for q in range(Q):
                    m = v.tensor_scalar(x1c[:, j % 4, q, :], y_tok[:, q, :], mv1[:, q, 0:1], rs1[:, 1, q:q + 1],
                                        ALU.subtract, ALU.mult)
                m.then_inc(x1_done, 1)

            v.wait_ge(ld_w, 16 * 14)
            v.wait_ge(w_col2, 1)
            v.tensor_scalar(td[:], ntd[:], -1.0, None, ALU.mult).then_inc(w_col2, 1)
            v.tensor_scalar(htf[:], tcol[:, 1, :], 0.5, None, ALU.mult).then_inc(w_col2, 1)
            v.tensor_scalar(omix[:], tcol[:, 2:5, :], -1.0, 1.0, ALU.mult, ALU.add).then_inc(w_col2, 1)
            v.wait_ge(w_cols, 16 * 3)
            v.tensor_scalar(wo[:], wo[:], 0.5, None, ALU.mult).then_inc(w_col2, 1)
            v.wait_ge(w_sum, 1)
            v.tensor_scalar(wmean[:], row_ps[:, 0, 0:2], 1.0 / (F * H), 1e-5, ALU.mult, ALU.max).then_inc(w_scl, 1)
            v.wait_ge(w_scl, 1)
            v.reciprocal(wscale[:], wmean[:]).then_inc(w_scl, 1)
            v.wait_ge(w_scl, 2)
            v.wait_ge(w_abs, 2)
            for n, (raw, tern) in enumerate(((w1_raw, w1T[:]), (w2_raw, w2_tern))):
                flat = lambda a: a.rearrange("p c h -> p (c h)")
                if n:
                    v.wait_ge(w_tern, 1)
                v.tensor_scalar(flat(tern), flat(raw), wscale[:, n:n + 1], 0.5, ALU.mult, ALU.is_gt).then_inc(w_scl, 1)
                v.tensor_scalar(tern_neg, flat(raw), wscale[:, n:n + 1], -0.5, ALU.mult, ALU.is_lt).then_inc(w_scl, 1)
                v.wait_ge(w_scl, 4 + 2 * n)
                v.tensor_tensor(flat(tern), flat(tern), tern_neg, ALU.subtract).then_inc(w_tern, 1)
            v.wait_ge(w_tern, 2)
            for f in range(FC):
                m = v.tensor_scalar(w2c[:, f, 0:H], w2_tern[:, f, :], fcol[:, 1, f:f + 1], None, ALU.mult)
            m.then_inc(w_tern, 1)
            v.wait_ge(s_const, 3)
            for f in range(FC):
                m = v.tensor_scalar(bias_rows[:, f, :], ones[:], fcol[:, 2, f:f + 1], None, ALU.mult)
            m.then_inc(w_bias, 1)
            v.memset(w2c[:, :, H:H + 1], 1.0).then_inc(w_rowc, 1)
            v.wait_ge(w_rows, 1)
            v.tensor_scalar(half_rows[:], row_ps[:, 1, 0:H], 1.0 / F, None, ALU.mult).then_inc(w_rowc, 1)
            v.tensor_scalar(const_row[:], row_ps[:, 0, 0:H], wmean[:, 1:2], None, ALU.mult).then_inc(w_rowc, 1)
            v.wait_ge(w_rowc, 3)
            v.wait_ge(w_tern, 3)
            v.tensor_tensor(const_row[:], row_ps[:, 1, H:2 * H], const_row[:], ALU.add).then_inc(w_rowc, 1)
            for f in range(FC):
                m = v.tensor_tensor(w2c[:, f, 0:H], w2c[:, f, 0:H], half_rows[:], ALU.subtract)
            m.then_inc(w_rowc, 1)
            v.wait_ge(w_rowc, 5)
            v.wait_ge(w_col2, 5)
            v.tensor_copy(rs1[:, 0, 0:1], wmean[:, 0:1]).then_inc(w_done, 1)
            mix(0, 0)

            def step(i, j, zs=2, has_next=True):
                wkv_a(i, 0)
                if zs:
                    z_part(i - 2, j + 2, first=zs == 1)
                wkv_b(i, 0)
                wkv_c(i, 0)
                wkv_a(i, 1)
                if zs:
                    z_end(i - 2)
                wkv_b(i, 1)
                wkv_c(i, 1)
                if has_next:
                    mix(i + 1, j + 1)
                ln1(i, j)

            for i in range(JT):
                step(i, i, zs=min(max(i - 1, 0), 2))
            with v.Fori(1, B - 1) as b:
                for j in range(JT):
                    step(b * JT + j, j)
            for i in range(NT - JT, NT):
                step(i, i % JT, has_next=i + 1 < NT)
            for i in (NT - 2, NT - 1):
                z_part(i, i % JT)
                z_end(i)

        @block.gpsimd
        def _(g):
            g.memset(z_tok[:, 0, :], 0.0).then_inc(s_const, 1)
            g.memset(ones[:], 1.0).then_inc(s_const, 1)
            g.memset(nhalf[:], -0.5).then_inc(s_const, 1)
            g.memset(ident[:], 0.0).then_inc(s_ident, 1)
            g.wait_ge(s_ident, 1)
            g.affine_select(out=ident[:], in_=ident[:], compare_op=ALU.not_equal, fill=1.0, base=0,
                            pattern=[[-1, P]], channel_multiplier=1).then_inc(s_ident, 1)
            g.memset(init[:, 1:4], 0.0).then_inc(s_ident, 1)
            g.memset(init[:, 0:1], NO_MAX).then_inc(s_ident, 1)
            g.memset(xT[:, 0, :, 0:1], 0.0).then_inc(xt_first, 1)
            g.wait_ge(xt_first, 1)
            g.wait_ge(s_ident, 4)

            def carry(i, new_sequence):
                for h in range(KC):
                    if not (isinstance(i, int) and i == 0):
                        g.wait_ge(rwkv_done, KC * i - 1 + h)
                        g.wait_ge(garg_done, KC * i - 1 + h)
                    src = init[:] if new_sequence else hist[:, h, :, TOK]
                    settled(g)
                    g.tensor_copy(hist[:, h, :, 0], src).then_inc(carried, 1)

            def keeps(i, j):
                g.wait_ge(ld_xT[j], (i - j) // JT * 32 + 32 if isinstance(i, int) else (i - j) * 8 + 32)
                for n in range(6):
                    w, c = n // KC, n % KC
                    if not (isinstance(i, int) and i == 0 and n < 2):
                        g.wait_ge(mix_done, 6 * i + n - 1)
                    settled(g)
                    g.tensor_scalar(keep[:, n % 2, :], xT[:, j, c, 0:TOK], omix[:, w, c:c + 1], 0.0,
                                    ALU.mult, ALU.add).then_inc(kept, 1)

            def wkv(i, h):
                n = KC * i + h
                d = dlt[:, h, :]
                g.wait_ge(dlt_done, n + 1)
                if not (isinstance(i, int) and i == 0):
                    g.wait_ge(den_done, n - 1)
                settled(g)
                g.tensor_scalar(e1[:, h, :], d, 3e38, td[:, h:h + 1], ALU.min, ALU.max).then_inc(m_done, 1)
                g.tensor_scalar(m2[:, h, :], d, td[:, h:h + 1], -3e38, ALU.min, ALU.max).then_inc(m_done, 1)
                g.wait_ge(ln_done, n + 1)
                g.wait_ge(m_done, 2 * n + 2)
                g.tensor_tensor(beta[:, h, :], m2[:, h, :], hist[:, h, 1, 1:TOK + 1], ALU.subtract).then_inc(barg_done, 1)
                g.tensor_tensor(dlt[:, h, :], d, hist[:, h, 1, 0:TOK], ALU.subtract).then_inc(garg_done, 1)
                g.wait_ge(beta_done, n + 1)
                settled(g)
                g.tensor_scalar(obeta[:, h, :], beta[:, h, :], -1.0, 1.0, ALU.mult, ALU.add).then_inc(obeta_done, 1)

            def rs_ln1(i):
                g.wait_ge(mv1_done, i + 1)
                if not (isinstance(i, int) and i == 0):
                    g.wait_ge(x1_done, i)
                s = 5 * i
                settled(g)
                g.tensor_scalar(rs1[:, 0, :], mv1[:, :, 1], EPS, 1.0, ALU.add, ALU.mult).then_inc(rs1_step, 1)
                g.wait_ge(rs1_step, s + 1)
                g.tensor_tensor(rs1[:, 1, :], rs1[:, 0, :], nhalf[:], ALU.pow).then_inc(rs1_step, 1)
                g.wait_ge(rs1_step, s + 2)
                g.tensor_tensor(rs1[:, 2, :], rs1[:, 1, :], mv1[:, :, 1], ALU.mult).then_inc(rs1_step, 1)
                g.wait_ge(rs1_step, s + 3)
                g.tensor_tensor(rs1[:, 3, :], rs1[:, 2, :], rs1[:, 1, :], ALU.mult).then_inc(rs1_step, 1)
                g.wait_ge(rs1_step, s + 4)
                settled(g)
                g.tensor_scalar(rs1[:, 3, :], rs1[:, 3, :], EPS, 1.0, ALU.add, ALU.mult).then_inc(rs1_step, 1)
                g.wait_ge(rs1_step, s + 5)
                g.tensor_tensor(rs1[:, 4, :], rs1[:, 3, :], nhalf[:], ALU.pow).then_inc(rs1_fine, 1)
                g.wait_ge(rs1_fine, i + 1)
                g.tensor_tensor(rs1[:, 5, :], rs1[:, 4, :], rs1[:, 1, :], ALU.mult).then_inc(rs1_done, 1)

            def add_const(i, j):
                g.wait_ge(x1_done, i + 1)
                for q in range(Q):
                    m = g.tensor_tensor(x1c[:, j % 4, q, :], x1c[:, j % 4, q, :], const_row[:], ALU.add)
                m.then_inc(x1c_done, 1)

            def rs_ln2(i):
                g.wait_ge(proj_done, Q * (i + 1))
                if not (isinstance(i, int) and i == 0):
                    g.wait_ge(z_done, Q * i)
                s = 6 * i
                settled(g)
                g.tensor_scalar(rs2[:, 0, :], proj[:, :, H], 1.0 / F, 0.0, ALU.mult, ALU.add).then_inc(rs2_step, 1)
                g.tensor_scalar(rs2[:, 1, :], proj[:, :, H + 1], 1.0 / F, 0.0, ALU.mult, ALU.add).then_inc(rs2_step, 1)
                g.wait_ge(rs2_step, s + 2)
                g.tensor_tensor(rs2[:, 2, :], rs2[:, 0, :], rs2[:, 0, :], ALU.mult).then_inc(rs2_step, 1)
                g.wait_ge(rs2_step, s + 3)
                g.tensor_tensor(rs2[:, 3, :], rs2[:, 1, :], rs2[:, 2, :], ALU.subtract).then_inc(rs2_step, 1)
                g.wait_ge(rs2_step, s + 4)
                settled(g)
                g.tensor_scalar(rs2[:, 4, :], rs2[:, 3, :], 0.0, EPS, ALU.max, ALU.add).then_inc(rs2_step, 1)
                g.wait_ge(rs2_step, s + 5)
                g.tensor_tensor(rs2[:, 5, :], rs2[:, 4, :], nhalf[:], ALU.pow).then_inc(rs2_step, 1)
                g.wait_ge(rs2_step, s + 6)
                settled(g)
                g.tensor_scalar(rs2[:, 6, :], rs2[:, 5, :], wmean[:, 1:2], 0.0, ALU.mult, ALU.add).then_inc(rs2_done, 1)

            def rs_ln3(i):
                g.wait_ge(mv3_done, i + 1)
                if not (isinstance(i, int) and i == 0):
                    g.wait_ge(fin_done, i)
                settled(g)
                g.tensor_scalar(rs3[:, 0, :], mv3[:, :, 1], EPS, 1.0, ALU.add, ALU.mult).then_inc(rs3_step, 1)
                g.wait_ge(rs3_step, i + 1)
                g.tensor_tensor(rs3[:, 1, :], rs3[:, 0, :], nhalf[:], ALU.pow).then_inc(rs3_done, 1)

            def step(i, j, zs=2, first=False, has_next=True):
                wkv(i, 0)
                if zs:
                    rs_ln3(i - 2)
                wkv(i, 1)
                if has_next:
                    keeps(i + 1, (j + 1) % JT)
                    carry(i + 1, j == JT - 1)
                rs_ln1(i)
                add_const(i, j)
                if not first:
                    rs_ln2(i - 1)

            g.wait_ge(w_done, 1)
            carry(0, True)
            keeps(0, 0)
            for i in range(JT):
                step(i, i, zs=min(max(i - 1, 0), 2), first=i == 0)
            with g.Fori(1, B - 1) as b:
                for j in range(JT):
                    step(b * JT + j, j)
            for i in range(NT - JT, NT):
                step(i, i % JT, has_next=i + 1 < NT)
            rs_ln3(NT - 2)
            rs_ln2(NT - 1)
            rs_ln3(NT - 1)


_INS = ["hidden", "Wk", "Wv", "Wr", "Wo", "time_decay", "time_first", "time_mix_key", "time_mix_value",
        "time_mix_receptance"]
_FFN = ["ln1_g", "ln1_b", "w1", "b1", "ln2_g", "ln2_b", "w2", "b2"]


def kernel(**inputs):
    import concourse.bacc as bacc
    from concourse.bass_utils import run_bass_kernel_spmd

    nc = bacc.Bacc("TRN2", target_bir_lowering=False, num_devices=1)
    names = [f"L0_attn_{n}" for n in _INS] + [f"L0_ffn_{n}" for n in _FFN]
    laid = {name: inputs[name] for name in names}
    for name in laid:
        a = np.asarray(laid[name])
        if name.endswith(("_w1", "_w2")):
            laid[name] = a.T
        elif a.ndim == 1 and not name.endswith("_b2"):
            laid[name] = a.reshape(-1, P).T
    hidden = laid.pop("L0_attn_hidden")
    laid = {"hidden": hidden, "hidden_by_channel": np.transpose(np.asarray(hidden), (0, 2, 1)), **laid}
    arrays, args = {}, []
    for name, a in laid.items():
        a = np.ascontiguousarray(a)
        arrays[f"in_{name}"] = a
        args.append(nc.dram_tensor(f"in_{name}", a.shape, mybir.dt.from_np(a.dtype), kind="ExternalInput").ap())
    shape = inputs["L0_attn_hidden"].shape
    args.append(nc.dram_tensor("out", shape, F32, kind="ExternalOutput").ap())
    build(nc, *args)
    return run_bass_kernel_spmd(nc, [arrays], core_ids=[0]).results[0]["out"]
```

```python
from contextlib import ExitStack

import numpy as np

import concourse.bass as bass
from concourse import mybir

F32 = mybir.dt.float32
BF16 = mybir.dt.bfloat16
F16 = mybir.dt.float16
ALU = mybir.AluOpType
ACT = mybir.ActivationFunctionType
AX = mybir.AxisListType

P = 128
TOK = 512
Q = TOK // P
EPS = 1e-5
NO_MAX = -1e38


def build(nc, x_in, x_by_channel, Wk, Wv, Wr, Wo, time_decay, time_first, mix_k, mix_v, mix_r,
          ln1_g, ln1_b, w1, b1, ln2_g, ln2_b, w2, b2, out):
    B, T, H = x_in.shape
    F = w1.shape[1]
    KC = H // P
    FC = F // P
    JT = T // TOK
    NT = B * JT
    assert H == KC * P and KC == 2 and F == FC * P and T == JT * TOK and Q == 4 and JT == 4

    x_rows = x_in.rearrange("b (j q p) h -> (b j) p q h", q=Q, p=P)
    x_cols = x_by_channel.rearrange("b (c p) t -> p b c t", p=P)
    out_rows = out.rearrange("b (j q p) h -> (b j) p q h", q=Q, p=P)

    with ExitStack() as ctx:
        def sb(name, shape, dtype=F32):
            return ctx.enter_context(nc.sbuf_tensor(name, shape, dtype))

        def ps(name, shape):
            return ctx.enter_context(nc.psum_tensor(name, shape, F32))

        def sem(name):
            return ctx.enter_context(nc.semaphore(name))

        ident = sb("ident", [P, P])
        ones = sb("ones", [P, P])
        wkvr = sb("wkvr", [P, 3, KC, H])
        wo = sb("wo", [P, KC, H])
        w1_hi = sb("w1_hi", [P, KC, F], BF16)
        w1_lo = sb("w1_lo", [P, KC, F], F16)
        w2c = sb("w2c", [P, FC, H + 1])
        tcol = sb("tcol", [P, 5, KC])
        ntd = sb("ntd", [P, KC])
        td = sb("td", [P, KC])
        htf = sb("htf", [P, KC])
        omix = sb("omix", [P, 3, KC])
        lncol = sb("lncol", [P, 2, KC])
        fcol = sb("fcol", [P, 3, FC])
        wabs = sb("wabs", [P, 2])
        wmean = sb("wmean", [P, 2])
        wscale = sb("wscale", [P, 2])
        const_row = sb("const_row", [P, H])
        half_rows = sb("half_rows", [P, H])
        init = sb("init", [P, 4])
        nhalf = sb("nhalf", [P, Q])

        x_tok = sb("x_tok", [P, 4, Q, H])
        xT = sb("xT", [P, JT, KC, TOK + 1])
        keep = sb("keep", [P, 2, TOK])
        mixed = sb("mixed", [P, 3, KC, TOK])
        hist = sb("hist", [P, KC, 4, TOK + 1])
        dlt = sb("dlt", [P, KC, TOK])
        e1 = sb("e1", [P, KC, TOK])
        e2 = sb("e2", [P, KC, TOK])
        m2 = sb("m2", [P, KC, TOK])
        beta = sb("beta", [P, KC, TOK])
        val = sb("val", [P, KC, TOK])
        wdf = sb("wdf", [P, KC, TOK])
        tr = sb("tr", [P, KC, TOK])
        rwkv = sb("rwkv", [P, KC, TOK])
        hn = sb("hn", [P, Q, H])
        x1c = sb("x1c", [P, 4, Q, H])
        hT = sb("hT", [P, KC, TOK])
        hT_hi = sb("hT_hi", [P, KC, TOK], BF16)
        hT_lo = sb("hT_lo", [P, KC, TOK], F16)
        u = sb("u", [P, FC, TOK])
        usq = sb("usq", [P, FC, TOK])
        proj = sb("proj", [P, Q, H + 1])
        sq_tok = sb("sq_tok", [P, Q])
        z_tok = sb("z_tok", [P, Q, H])
        bn1 = sb("bn1", [P, Q, 6])
        mv1 = sb("mv1", [P, Q, 2])
        rs1 = sb("rs1", [P, 6, Q])
        rs2 = sb("rs2", [P, 8, Q])
        bn3 = sb("bn3", [P, Q, 6])
        mv3 = sb("mv3", [P, Q, 2])
        rs3 = sb("rs3", [P, 2, Q])

        kvr_ps = ps("kvr_ps", [P, 3, 512])
        up_ps = ps("up_ps", [P, 2, 512])
        row_ps = ps("row_ps", [P, 2, 512])
        sum_ps = ps("sum_ps", [P, 512])

        ld_w = sem("ld_w"); ld_wkvr = sem("ld_wkvr"); ld_ffn = sem("ld_ffn"); ld_w12 = sem("ld_w12"); ld_xT = [sem(f"ld_xT{b}") for b in range(4)]; ld_x = [sem(f"ld_x{b}") for b in range(4)]
        st_out = sem("st_out")
        s_passed = sem("s_passed"); s_const = sem("s_const"); s_ident = sem("s_ident")
        w_cols = sem("w_cols"); w_ntd = sem("w_ntd"); s_zero = sem("s_zero")
        w_abs = sem("w_abs"); w_sum = sem("w_sum"); w_scl = sem("w_scl"); w_tern = sem("w_tern"); w_lo = sem("w_lo")
        w_bias = sem("w_bias")
        w_rows = sem("w_rows"); w_rowc = sem("w_rowc"); w_done = sem("w_done")
        xt_first = sem("xt_first"); v_done = sem("v_done"); split_hi = sem("split_hi"); split_done = sem("split_done")
        folded = sem("folded"); sums_ready = sem("sums_ready"); sums_done = sem("sums_done")
        kept = sem("kept"); mix_done = sem("mix_done")
        k_ready = sem("k_ready"); v_ready = sem("v_ready"); r_ready = sem("r_ready"); carried = sem("carried")
        mx_done = sem("mx_done"); dlt_done = sem("dlt_done")
        m_done = sem("m_done"); e_done = sem("e_done"); den_done = sem("den_done")
        ln_done = sem("ln_done"); barg_done = sem("barg_done"); garg_done = sem("garg_done")
        beta_done = sem("beta_done"); obeta_done = sem("obeta_done"); bv_done = sem("bv_done")
        avg_done = sem("avg_done"); wdf_done = sem("wdf_done"); gam_done = sem("gam_done")
        tr_done = sem("tr_done"); g1_done = sem("g1_done"); o1_done = sem("o1_done")
        rwkv_done = sem("rwkv_done")
        att_ready = sem("att_ready"); y_done = sem("y_done"); bn1_done = sem("bn1_done")
        mv1_done = sem("mv1_done"); rs1_step = sem("rs1_step"); rs1_fine = sem("rs1_fine"); rs1_done = sem("rs1_done")
        x1_done = sem("x1_done"); hn_done = sem("hn_done"); x1c_done = sem("x1c_done")
        ht_ready = sem("ht_ready"); ht_evac = sem("ht_evac")
        up_ready = sem("up_ready"); u_done = sem("u_done"); usq_done = sem("usq_done")
        down_ready = sem("down_ready"); proj_done = sem("proj_done")
        rs2_step = sem("rs2_step"); rs2_done = sem("rs2_done")
        z_done = sem("z_done"); bn3_done = sem("bn3_done"); mv3_done = sem("mv3_done")
        rs3_step = sem("rs3_step"); rs3_done = sem("rs3_done"); fin_done = sem("fin_done")

        obeta, bv = m2, e1
        flat_u, flat_usq = (a[:].rearrange("p c t -> p (c t)") for a in (u, usq))
        flat_x1c = x1c[:].rearrange("p b q h -> p (b q h)")
        w1_raw = flat_u[:, 0:FC * H]
        w2_raw = flat_u[:, FC * H:2 * FC * H]
        tern_pos, tern_neg = flat_usq[:, 0:FC * H], flat_usq[:, FC * H:2 * FC * H]
        w2_tern = flat_x1c[:, 0:FC * H]
        bias_rows = flat_x1c[:, FC * H:FC * H + FC * P].rearrange("p (c m) -> p c m", c=FC)
        b2_row = z_tok[:, 0, :]

        def here(i):
            return not isinstance(i, int) or 0 <= i < NT

        def later(i):
            return not isinstance(i, int) or i > 0

        def rounds(i, j, each):
            return (i - j) // JT * each + each if isinstance(i, int) else (i - j) * (each // JT) + each

        def steps(run, eng):
            for i in range(JT):
                run(i, i)
            with eng.Fori(1, B - 1) as b:
                for j in range(JT):
                    run(b * JT + j, j)
            for i in range(NT - JT, NT + 3):
                run(i, i % JT)

        block = ctx.enter_context(nc.Block())

        def settled(eng):
            eng.sem_inc(s_passed, 1)

        @block.sync
        def _(sp):
            def load(i, j, b):
                sp.dma_start(x_tok[:, j], x_rows[i]).then_inc(ld_x[j], 16)
                for c in range(KC):
                    if j == 0:
                        sp.dma_start(xT[:, 0, c, 1:TOK + 1], x_cols[:, b, c, 0:TOK]).then_inc(ld_xT[0], 16)
                    else:
                        sp.dma_start(xT[:, j, c, :], x_cols[:, b, c, j * TOK - 1:(j + 1) * TOK]).then_inc(ld_xT[j], 16)

            for n, vec in enumerate((time_decay, time_first, mix_k, mix_v, mix_r)):
                sp.dma_start(tcol[:, n, :], vec).then_inc(ld_w, 16)
            load(0, 0, 0)
            for n, w in enumerate((Wk, Wv, Wr)):
                sp.dma_start(wkvr[:, n], w.rearrange("(c p) n -> p c n", p=P)).then_inc(ld_wkvr, 16)
            sp.dma_start(w1_raw.rearrange("p (c f) -> p c f", c=KC), w1.rearrange("(c p) n -> p c n", p=P)).then_inc(ld_w12, 16)
            sp.dma_start(w2_raw.rearrange("p (c h) -> p c h", c=FC), w2.rearrange("(c p) n -> p c n", p=P)).then_inc(ld_w12, 16)
            for n, vec in enumerate((ln1_g, ln1_b)):
                sp.dma_start(lncol[:, n, :], vec).then_inc(ld_ffn, 16)
            for n, vec in enumerate((b1, ln2_g, ln2_b)):
                sp.dma_start(fcol[:, n, :], vec).then_inc(ld_ffn, 16)
            sp.dma_start(wo[:], Wo.rearrange("(c p) n -> p c n", p=P)).then_inc(ld_ffn, 16)
            sp.wait_ge(s_const, 1)
            sp.dma_start(b2_row[0:1, :], b2.rearrange("(a n) -> a n", a=1)).then_inc(ld_ffn, 16)
            for j in range(1, JT):
                load(j, j, 0)

            def step(i, j, b):
                if i is not None and here(i + 3):
                    sp.wait_ge(x1_done, i)
                    settled(sp)
                    sp.wait_ge(mix_done, 6 * i)
                    settled(sp)
                    load(i + 3, (j + 3) % JT, b if j == 0 else b + 1)
                if here(i - 3):
                    sp.wait_ge(fin_done, i - 2)
                    settled(sp)
                    sp.dma_start(out_rows[i - 3], z_tok[:]).then_inc(st_out, 16)

            for i in range(1, JT):
                step(i, i, 0)
            with sp.Fori(1, B - 1) as b:
                for j in range(JT):
                    step(b * JT + j, j, b)
            for i in range(NT - JT, NT + 3):
                step(i, i % JT, i // JT)
            sp.wait_ge(st_out, 16 * NT)

        @block.tensor
        def _(pe):
            def kvr(i):
                to_k, to_v, to_r = (0, dlt_done, k_ready), (1, v_done, v_ready), (2, tr_done, r_ready)
                for h in range(KC):
                    n = KC * i + h
                    for w, used, ready in ((to_k, to_v, to_r), (to_v, to_k, to_r))[h]:
                        if h == 0:
                            pe.wait_ge(mix_done, 6 * i + 2 * (w + 1))
                        if later(n):
                            pe.wait_ge(used, n)
                        for c in range(KC):
                            m = pe.matmul(kvr_ps[:, w, :], wkvr[:, w, c, h * P:(h + 1) * P],
                                          mixed[:, w, c, :], start=(c == 0), stop=(c == KC - 1))
                        m.then_inc(ready, 1)

            def turn_h(i):
                pe.wait_ge(hn_done, i + 1)
                if later(i):
                    pe.wait_ge(u_done, FC * i)
                for c in range(KC):
                    for q in range(Q):
                        m = pe.transpose(up_ps[:, c, q * P:(q + 1) * P], hn[:, q, c * P:(c + 1) * P], ident[:])
                    m.then_inc(ht_ready, 1)

            def att(i):
                pe.wait_ge(rwkv_done, KC * (i + 1))
                if later(i - 1):
                    pe.wait_ge(proj_done, Q * (i - 1))
                for g in range(2):
                    for q in range(2):
                        t = slice((2 * g + q) * P, (2 * g + q + 1) * P)
                        for c in range(KC):
                            m = pe.matmul(row_ps[:, g, q * H:(q + 1) * H], rwkv[:, c, t], wo[:, c, :],
                                          start=(c == 0), stop=(c == KC - 1))
                    m.then_inc(att_ready, 1)

            def sums(i):
                pe.wait_ge(folded, 3 * i + 3)
                if later(i):
                    pe.wait_ge(sums_done, i)
                for q in range(Q):
                    m = pe.matmul(sum_ps[:, q:q + 1], usq[:, 0, q * P:(q + 1) * P], ones[:, 0:1],
                                  start=True, stop=True)
                m.then_inc(sums_ready, 1)

            def up(i):
                pe.wait_ge(split_done, KC * (i + 1))
                for f in range(FC):
                    if f >= 2:
                        pe.wait_ge(u_done, FC * i + f - 1)
                    k = 0
                    for w, part in ((w1_hi, hT_hi), (w1_lo, hT_lo)):
                        for c in range(KC):
                            m = pe.matmul(up_ps[:, f % 2, :], w[:, c, f * P:(f + 1) * P], part[:, c, :],
                                          start=(k == 0), stop=(k == 3))
                            k += 1
                    m.then_inc(up_ready, 1)

            def down(i):
                if here(i + 1):
                    pe.wait_ge(y_done, 2 * (i + 2))
                for q in range(Q):
                    if q >= 2 or not here(i + 1):
                        pe.wait_ge(proj_done, Q * i + q - 1)
                    for f in range(FC):
                        if q == 0:
                            pe.wait_ge(u_done, FC * i + f + 1)
                        m = pe.matmul(row_ps[:, q % 2, 0:H + 1], u[:, f, q * P:(q + 1) * P], w2c[:, f, :],
                                      start=(f == 0), stop=(f == FC - 1))
                    m.then_inc(down_ready, 1)

            def weight_sums():
                pe.wait_ge(s_const, 2)
                pe.wait_ge(w_abs, 2)
                pe.matmul(sum_ps[:, 0:2], ones[:], wabs[:], start=True, stop=True).then_inc(w_sum, 1)

            def weight_rows():
                pe.wait_ge(w_bias, 1)
                pe.wait_ge(w_tern, 3)
                pe.wait_ge(ld_ffn, 16 * 7)
                for f in range(FC):
                    pe.matmul(up_ps[:, 0, 0:H], bias_rows[:, f, :], w2_tern[:, f * H:(f + 1) * H],
                              start=(f == 0), stop=(f == FC - 1))
                for f in range(FC):
                    pe.matmul(up_ps[:, 1, 0:H], ones[:], w2c[:, f, 0:H],
                              start=(f == 0), stop=(f == FC - 1))
                pe.matmul(up_ps[:, 1, H:2 * H], ones[:], b2_row, start=True, stop=True).then_inc(w_rows, 1)

            def step(i, j):
                if here(i):
                    kvr(i)
                if isinstance(i, int) and i == 0:
                    weight_sums()
                if isinstance(i, int) and i == 1:
                    weight_rows()
                if here(i - 2):
                    turn_h(i - 2)
                if here(i - 1):
                    att(i - 1)
                if here(i - 3):
                    sums(i - 3)
                if here(i - 2):
                    up(i - 2)
                    down(i - 2)
                if isinstance(i, int) and i == 1:
                    pe.wait_ge(w_done, 1)
                    pe.wait_ge(s_ident, 2)

            pe.wait_ge(ld_wkvr, 48)
            steps(step, pe)

        @block.scalar
        def _(act):
            def wkv_weights(i):
                for h in range(KC):
                    n = KC * i + h
                    act.wait_ge(v_ready, n + 1)
                    if later(i):
                        act.wait_ge(rwkv_done, n - 1)
                    act.activation(val[:, h, :], kvr_ps[:, 1, :], ACT.Copy).then_inc(v_done, 1)
                    act.wait_ge(r_ready, n + 1)
                    act.activation(tr[:, h, :], kvr_ps[:, 2, :], ACT.Tanh, scale=0.5).then_inc(tr_done, 1)
                    act.wait_ge(m_done, 2 * n + 1)
                    act.activation(e1[:, h, :], e1[:, h, :], ACT.Exp, bias=td[:, h:h + 1], scale=-1.0).then_inc(e_done, 1)
                    act.wait_ge(m_done, 2 * n + 2)
                    act.activation(e2[:, h, :], m2[:, h, :], ACT.Exp, bias=ntd[:, h:h + 1]).then_inc(e_done, 1)

            def evac_h(i):
                if later(i):
                    act.wait_ge(split_done, KC * i)
                for c in range(KC):
                    act.wait_ge(ht_ready, KC * i + c + 1)
                    act.activation(hT[:, c, :], up_ps[:, c, :], ACT.Identity, bias=lncol[:, 1, c:c + 1],
                                   scale=lncol[:, 0, c:c + 1]).then_inc(ht_evac, 1)

            def ln_den(i):
                for h in range(KC):
                    act.wait_ge(den_done, KC * i + h + 1)
                    act.activation(hist[:, h, 1, 1:TOK + 1], hist[:, h, 3, 1:TOK + 1], ACT.Ln).then_inc(ln_done, 1)

            def copy_sums(i):
                act.wait_ge(sums_ready, i + 1)
                if later(i):
                    act.wait_ge(rs2_done, i)
                act.activation(sq_tok[:], sum_ps[:, 0:Q], ACT.Copy).then_inc(sums_done, 1)

            def gelus(i):
                if later(i):
                    act.wait_ge(down_ready, Q * i)
                for f in range(FC):
                    act.wait_ge(up_ready, FC * i + f + 1)
                    act.activation(u[:, f, :], up_ps[:, f % 2, :], ACT.Gelu, bias=fcol[:, 0, f:f + 1],
                                   scale=wmean[:, 0:1]).then_inc(u_done, 1)

            def beta_gamma(i):
                for h in range(KC):
                    n = KC * i + h
                    act.wait_ge(barg_done, n + 1)
                    act.activation(beta[:, h, :], beta[:, h, :], ACT.Exp, bias=ntd[:, h:h + 1]).then_inc(beta_done, 1)
                    act.wait_ge(garg_done, n + 1)
                    act.activation(dlt[:, h, :], dlt[:, h, :], ACT.Tanh, bias=htf[:, h:h + 1], scale=0.5).then_inc(gam_done, 1)

            def copy_down(i, q):
                if later(i):
                    act.wait_ge(z_done, Q * i)
                act.wait_ge(down_ready, Q * i + q + 1)
                act.activation(proj[:, q, :], row_ps[:, q % 2, 0:H + 1], ACT.Copy).then_inc(proj_done, 1)

            def squares(i, f0, f1):
                if later(i):
                    act.wait_ge(sums_ready, i)
                for f in range(f0, f1):
                    act.wait_ge(u_done, FC * i + f + 1)
                    act.activation(usq[:, f, :], u[:, f, :], ACT.Square).then_inc(usq_done, 1)

            def step(i, j):
                if here(i):
                    wkv_weights(i)
                if here(i - 2):
                    evac_h(i - 2)
                if here(i):
                    ln_den(i)
                if here(i - 3):
                    copy_sums(i - 3)
                if here(i - 2):
                    gelus(i - 2)
                if here(i):
                    beta_gamma(i)
                if here(i - 2):
                    copy_down(i - 2, 0)
                    squares(i - 2, 0, FC // 2)
                    copy_down(i - 2, 1)
                    squares(i - 2, FC // 2, FC)
                    copy_down(i - 2, 2)
                    copy_down(i - 2, 3)
                if isinstance(i, int) and i == 0:
                    act.wait_ge(w_tern, 1)
                    act.activation(w1_lo[:], w1_hi[:], ACT.Copy).then_inc(w_lo, 1)
                if isinstance(i, int) and i == 1:
                    act.wait_ge(w_done, 1)

            act.wait_ge(ld_w, 16 * 5)
            act.activation(ntd[:], tcol[:, 0, :], ACT.Exp).then_inc(w_ntd, 1)
            act.wait_ge(w_cols, 3)
            act.wait_ge(ld_w12, 16 * 2)
            act.activation(tern_pos, w1_raw, ACT.Abs, accum_out=wabs[:, 0:1]).then_inc(w_abs, 1)
            act.activation(tern_neg, w2_raw, ACT.Abs, accum_out=wabs[:, 1:2]).then_inc(w_abs, 1)
            steps(step, act)

        @block.vector
        def _(v):
            def wkv_a(i, h):
                n = KC * i + h
                k = kvr_ps[:, 0, :]
                d = dlt[:, h, :]
                v.wait_ge(k_ready, n + 1)
                v.wait_ge(carried, n + 1)
                v.tensor_tensor_scan(hist[:, h, 0, 1:TOK + 1], td[:, h:h + 1].broadcast_to([P, TOK]), k,
                                     hist[:, h, 0, 0:1], ALU.add, ALU.max).then_inc(mx_done, 1)
                v.wait_ge(mx_done, n + 1)
                v.tensor_tensor(d, k, hist[:, h, 0, 0:TOK], ALU.subtract).then_inc(dlt_done, 1)
                v.wait_ge(dlt_done, n + 1)
                v.tensor_scalar(e1[:, h, :], d, td[:, h:h + 1], None, ALU.max).then_inc(m_done, 1)
                v.tensor_scalar(m2[:, h, :], d, td[:, h:h + 1], None, ALU.min).then_inc(m_done, 1)

            def wkv_b(i, h):
                n = KC * i + h
                v.wait_ge(e_done, 2 * n + 2)
                v.tensor_tensor_scan(hist[:, h, 3, 1:TOK + 1], e1[:, h, :], e2[:, h, :],
                                     hist[:, h, 3, 0:1], ALU.mult, ALU.add).then_inc(den_done, 1)

            def wkv_c(i, j, h):
                n = KC * i + h
                v.wait_ge(v_done, n + 1)
                v.wait_ge(beta_done, n + 1)
                v.tensor_tensor(bv[:, h, :], val[:, h, :], beta[:, h, :], ALU.mult).then_inc(bv_done, 1)
                v.wait_ge(bv_done, n + 1)
                v.wait_ge(obeta_done, n + 1)
                v.tensor_tensor_scan(hist[:, h, 2, 1:TOK + 1], obeta[:, h, :], bv[:, h, :],
                                     hist[:, h, 2, 0:1], ALU.mult, ALU.add).then_inc(avg_done, 1)
                v.wait_ge(avg_done, n + 1)
                v.tensor_tensor(wdf[:, h, :], val[:, h, :], hist[:, h, 2, 0:TOK], ALU.subtract).then_inc(wdf_done, 1)
                v.wait_ge(wdf_done, n + 1)
                v.wait_ge(gam_done, n + 1)
                v.scalar_tensor_tensor(out=wdf[:, h, :], in0=dlt[:, h, :], scalar=1.0, in1=wdf[:, h, :],
                                       op0=ALU.add, op1=ALU.mult).then_inc(g1_done, 1)
                v.wait_ge(g1_done, n + 1)
                v.scalar_tensor_tensor(out=wdf[:, h, :], in0=wdf[:, h, :], scalar=0.5, in1=hist[:, h, 2, 0:TOK],
                                       op0=ALU.mult, op1=ALU.add).then_inc(o1_done, 1)
                v.wait_ge(o1_done, n + 1)
                v.wait_ge(tr_done, n + 1)
                if later(i):
                    v.wait_ge(att_ready, 2 * i)
                v.scalar_tensor_tensor(out=rwkv[:, h, :], in0=tr[:, h, :], scalar=1.0, in1=wdf[:, h, :],
                                       op0=ALU.add, op1=ALU.mult).then_inc(rwkv_done, 1)
                v.wait_ge(garg_done, n + 1)
                src = init[:] if j == JT - 1 else hist[:, h, :, TOK]
                v.tensor_copy(hist[:, h, :, 0], src).then_inc(carried, 1)

            def mix(i, j):
                if later(i):
                    v.wait_ge(r_ready, KC * i)
                for n in range(6):
                    w, c = n // KC, n % KC
                    v.wait_ge(kept, 6 * i + n + 1)
                    v.scalar_tensor_tensor(out=mixed[:, w, c, :], in0=xT[:, j, c, 1:TOK + 1],
                                           scalar=tcol[:, 2 + w, c:c + 1], in1=keep[:, n % 2, :],
                                           op0=ALU.mult, op1=ALU.add).then_inc(mix_done, 1)

            def split_h(i):
                if later(i):
                    v.wait_ge(up_ready, FC * i)
                for c in range(KC):
                    v.wait_ge(ht_evac, KC * i + c + 1)
                    v.tensor_copy(hT_hi[:, c, :], hT[:, c, :]).then_inc(split_hi, 1)
                    v.wait_ge(split_hi, KC * i + c + 1)
                    v.tensor_tensor(hT_lo[:, c, :], hT[:, c, :], hT_hi[:, c, :], ALU.subtract).then_inc(split_done, 1)

            def residual(i, j):
                v.wait_ge(ld_x[j], rounds(i, j, 16))
                y = x_tok[:, j].rearrange("p (g q) h -> p g (q h)", g=2)
                for g in range(2):
                    v.wait_ge(att_ready, 2 * i + g + 1)
                    v.tensor_tensor(y[:, g], row_ps[:, g, :], y[:, g], ALU.add).then_inc(y_done, 1)
                for q in range(Q):
                    v.wait_ge(y_done, 2 * i + q // 2 + 1)
                    m = v.bn_stats(bn1[:, q, :], x_tok[:, j, q, :])
                m.then_inc(bn1_done, 1)
                v.wait_ge(bn1_done, i + 1)
                settled(v)
                for q in range(Q):
                    m = v.bn_aggr(mv1[:, q, :], bn1[:, q, :])
                m.then_inc(mv1_done, 1)

            def norm1(i, j):
                v.wait_ge(mv1_done, i + 1)
                v.wait_ge(rs1_done, i + 1)
                if later(i):
                    v.wait_ge(ht_ready, KC * i)
                for q in range(Q):
                    m = v.tensor_scalar(hn[:, q, :], x_tok[:, j, q, :], mv1[:, q, 0:1], rs1[:, 5, q:q + 1],
                                        ALU.subtract, ALU.mult)
                m.then_inc(hn_done, 1)
                for q in range(Q):
                    m = v.tensor_scalar(x1c[:, j, q, :], x_tok[:, j, q, :], mv1[:, q, 0:1], rs1[:, 1, q:q + 1],
                                        ALU.subtract, ALU.mult)
                m.then_inc(x1_done, 1)

            def z_part(i, j):
                if later(i):
                    v.wait_ge(st_out, 16 * i)
                v.wait_ge(x1c_done, i + 1)
                v.wait_ge(rs2_done, i + 1)
                for q in range(Q):
                    v.scalar_tensor_tensor(out=z_tok[:, q, :], in0=proj[:, q, 0:H], scalar=rs2[:, 6, q:q + 1],
                                           in1=x1c[:, j, q, :], op0=ALU.mult, op1=ALU.add).then_inc(z_done, 1)
                for q in range(Q):
                    v.wait_ge(z_done, Q * i + q + 1)
                    m = v.bn_stats(bn3[:, q, :], z_tok[:, q, :])
                m.then_inc(bn3_done, 1)
                v.wait_ge(bn3_done, i + 1)
                settled(v)
                for q in range(Q):
                    m = v.bn_aggr(mv3[:, q, :], bn3[:, q, :])
                m.then_inc(mv3_done, 1)

            def z_end(i):
                v.wait_ge(mv3_done, i + 1)
                v.wait_ge(rs3_done, i + 1)
                for q in range(Q):
                    m = v.tensor_scalar(z_tok[:, q, :], z_tok[:, q, :], mv3[:, q, 0:1], rs3[:, 1, q:q + 1],
                                        ALU.subtract, ALU.mult)
                m.then_inc(fin_done, 1)

            def weights_a():
                v.wait_ge(ld_ffn, 16 * 7)
                v.tensor_scalar(wo[:], wo[:], 0.5, None, ALU.mult)
                v.wait_ge(w_sum, 1)
                v.tensor_scalar(wmean[:], sum_ps[:, 0:2], 1.0 / (F * H), 1e-5, ALU.mult, ALU.max).then_inc(w_scl, 1)
                v.wait_ge(w_scl, 1)
                v.reciprocal(wscale[:], wmean[:]).then_inc(w_scl, 1)
                v.wait_ge(w_scl, 2)
                v.wait_ge(w_abs, 2)
                w1_flat = w1_hi[:].rearrange("p c f -> p (c f)")
                for n, (raw, tern) in enumerate(((w1_raw, w1_flat), (w2_raw, w2_tern))):
                    if n:
                        v.wait_ge(w_tern, 1)
                    v.tensor_scalar(tern_pos, raw, wscale[:, n:n + 1], 0.5, ALU.mult, ALU.is_gt).then_inc(w_scl, 1)
                    v.tensor_scalar(tern_neg, raw, wscale[:, n:n + 1], -0.5, ALU.mult, ALU.is_lt).then_inc(w_scl, 1)
                    v.wait_ge(w_scl, 4 + 2 * n)
                    v.tensor_tensor(tern, tern_pos, tern_neg, ALU.subtract).then_inc(w_tern, 1)
                v.wait_ge(w_tern, 2)
                for f in range(FC):
                    m = v.tensor_scalar(w2c[:, f, 0:H], w2_tern[:, f * H:(f + 1) * H], fcol[:, 1, f:f + 1], None, ALU.mult)
                m.then_inc(w_tern, 1)
                v.wait_ge(s_const, 2)
                for f in range(FC):
                    m = v.tensor_scalar(bias_rows[:, f, :], ones[:], fcol[:, 2, f:f + 1], None, ALU.mult)
                m.then_inc(w_bias, 1)
                v.memset(w2c[:, :, H:H + 1], 1.0).then_inc(w_rowc, 1)

            def weights_b():
                v.wait_ge(w_rows, 1)
                v.tensor_scalar(half_rows[:], up_ps[:, 1, 0:H], 1.0 / F, None, ALU.mult).then_inc(w_rowc, 1)
                v.tensor_scalar(const_row[:], up_ps[:, 0, 0:H], wmean[:, 1:2], None, ALU.mult).then_inc(w_rowc, 1)
                v.wait_ge(w_rowc, 3)
                v.wait_ge(w_tern, 3)
                v.tensor_tensor(const_row[:], up_ps[:, 1, H:2 * H], const_row[:], ALU.add).then_inc(w_rowc, 1)
                for f in range(FC):
                    m = v.tensor_tensor(w2c[:, f, 0:H], w2c[:, f, 0:H], half_rows[:], ALU.subtract)
                m.then_inc(w_rowc, 1)
                v.wait_ge(w_rowc, 5)
                v.wait_ge(w_bias, 1)
                v.wait_ge(w_lo, 1)
                v.tensor_copy(init[:, 0:1], init[:, 0:1]).then_inc(w_done, 1)

            def step(i, j):
                if here(i):
                    wkv_a(i, 0)
                    wkv_a(i, 1)
                    wkv_b(i, 0)
                    wkv_b(i, 1)
                if isinstance(i, int) and i == 0:
                    mix(1, 1)
                    weights_a()
                if here(i - 2):
                    split_h(i - 2)
                if here(i - 1):
                    residual(i - 1, (j - 1) % JT)
                if here(i - 3):
                    z_part(i - 3, (j - 3) % JT)
                if here(i - 1):
                    norm1(i - 1, (j - 1) % JT)
                if here(i + 1) and later(i):
                    mix(i + 1, (j + 1) % JT)
                if here(i - 3):
                    z_end(i - 3)
                if isinstance(i, int) and i == 1:
                    weights_b()
                if here(i):
                    wkv_c(i, j, 0)
                    wkv_c(i, j, 1)

            v.wait_ge(ld_w, 16 * 5)
            v.tensor_scalar(omix[:], tcol[:, 2:5, :], -1.0, 1.0, ALU.mult, ALU.add).then_inc(w_cols, 1)
            v.tensor_scalar(htf[:], tcol[:, 1, :], 0.5, None, ALU.mult).then_inc(w_cols, 1)
            v.wait_ge(w_ntd, 1)
            v.tensor_scalar(td[:], ntd[:], -1.0, None, ALU.mult).then_inc(w_cols, 1)
            v.wait_ge(s_ident, 4)
            for h in range(KC):
                v.tensor_copy(hist[:, h, :, 0], init[:]).then_inc(carried, 1)
            v.wait_ge(w_cols, 3)
            v.wait_ge(carried, 2)
            mix(0, 0)
            steps(step, v)

        @block.gpsimd
        def _(g):
            g.memset(z_tok[:, 0, :], 0.0).then_inc(s_const, 1)
            g.memset(ones[:], 1.0).then_inc(s_const, 1)
            g.memset(nhalf[:], -0.5).then_inc(s_ident, 1)
            g.memset(init[:, 1:4], 0.0).then_inc(s_ident, 1)
            g.memset(init[:, 0:1], NO_MAX).then_inc(s_ident, 1)
            g.memset(ident[:], 0.0).then_inc(s_zero, 1)
            g.memset(xT[:, 0, :, 0:1], 0.0).then_inc(xt_first, 1)
            g.wait_ge(s_zero, 1)
            g.affine_select(out=ident[:], in_=ident[:], compare_op=ALU.not_equal, fill=1.0, base=0,
                            pattern=[[-1, P]], channel_multiplier=1).then_inc(s_ident, 1)
            g.wait_ge(s_ident, 4)
            g.wait_ge(xt_first, 1)
            g.wait_ge(w_cols, 3)

            def fold(i, stage):
                half = FC >> (stage + 1)
                if stage == 0:
                    g.wait_ge(usq_done, FC * (i + 1))
                else:
                    g.wait_ge(folded, 3 * i + stage)
                g.tensor_tensor(usq[:, 0:half, :], usq[:, 0:half, :], usq[:, half:2 * half, :], ALU.add).then_inc(folded, 1)

            def keeps(i, j, n0, n1):
                g.wait_ge(ld_xT[j], rounds(i, j, 32))
                for n in range(n0, n1):
                    w, c = n // KC, n % KC
                    if later(i) or n >= 2:
                        g.wait_ge(mix_done, 6 * i + n - 1)
                    settled(g)
                    g.tensor_scalar(keep[:, n % 2, :], xT[:, j, c, 0:TOK], omix[:, w, c:c + 1], 0.0,
                                    ALU.mult, ALU.add).then_inc(kept, 1)

            def beta_arg(i, h):
                n = KC * i + h
                g.wait_ge(ln_done, n + 1)
                g.tensor_tensor(beta[:, h, :], m2[:, h, :], hist[:, h, 1, 1:TOK + 1], ALU.subtract).then_inc(barg_done, 1)

            def gamma_arg(i, h):
                n = KC * i + h
                g.wait_ge(m_done, 2 * n + 2)
                g.tensor_tensor(dlt[:, h, :], dlt[:, h, :], hist[:, h, 1, 0:TOK], ALU.subtract).then_inc(garg_done, 1)

            def other_beta(i, h):
                n = KC * i + h
                g.wait_ge(beta_done, n + 1)
                settled(g)
                g.tensor_scalar(obeta[:, h, :], beta[:, h, :], -1.0, 1.0, ALU.mult, ALU.add).then_inc(obeta_done, 1)

            def rs_ln1(i):
                g.wait_ge(mv1_done, i + 1)
                if later(i):
                    g.wait_ge(x1_done, i)
                s = 5 * i
                settled(g)
                g.tensor_scalar(rs1[:, 0, :], mv1[:, :, 1], EPS, 1.0, ALU.add, ALU.mult).then_inc(rs1_step, 1)
                g.wait_ge(rs1_step, s + 1)
                g.tensor_tensor(rs1[:, 1, :], rs1[:, 0, :], nhalf[:], ALU.pow).then_inc(rs1_step, 1)
                g.wait_ge(rs1_step, s + 2)
                g.tensor_tensor(rs1[:, 2, :], rs1[:, 1, :], mv1[:, :, 1], ALU.mult).then_inc(rs1_step, 1)
                g.wait_ge(rs1_step, s + 3)
                g.tensor_tensor(rs1[:, 3, :], rs1[:, 2, :], rs1[:, 1, :], ALU.mult).then_inc(rs1_step, 1)
                g.wait_ge(rs1_step, s + 4)
                settled(g)
                g.tensor_scalar(rs1[:, 3, :], rs1[:, 3, :], EPS, 1.0, ALU.add, ALU.mult).then_inc(rs1_step, 1)
                g.wait_ge(rs1_step, s + 5)
                g.tensor_tensor(rs1[:, 4, :], rs1[:, 3, :], nhalf[:], ALU.pow).then_inc(rs1_fine, 1)
                g.wait_ge(rs1_fine, i + 1)
                g.tensor_tensor(rs1[:, 5, :], rs1[:, 4, :], rs1[:, 1, :], ALU.mult).then_inc(rs1_done, 1)

            def add_const(i, j):
                g.wait_ge(x1_done, i + 1)
                for q in range(Q):
                    m = g.tensor_tensor(x1c[:, j, q, :], x1c[:, j, q, :], const_row[:], ALU.add)
                m.then_inc(x1c_done, 1)

            def rs_ln2(i):
                g.wait_ge(proj_done, Q * (i + 1))
                g.wait_ge(sums_done, i + 1)
                if later(i):
                    g.wait_ge(z_done, Q * i)
                s = 6 * i
                settled(g)
                g.tensor_scalar(rs2[:, 0, :], proj[:, :, H], 1.0 / F, 0.0, ALU.mult, ALU.add).then_inc(rs2_step, 1)
                g.tensor_scalar(rs2[:, 1, :], sq_tok[:], 1.0 / F, 0.0, ALU.mult, ALU.add).then_inc(rs2_step, 1)
                g.wait_ge(rs2_step, s + 2)
                g.tensor_tensor(rs2[:, 2, :], rs2[:, 0, :], rs2[:, 0, :], ALU.mult).then_inc(rs2_step, 1)
                g.wait_ge(rs2_step, s + 3)
                g.tensor_tensor(rs2[:, 3, :], rs2[:, 1, :], rs2[:, 2, :], ALU.subtract).then_inc(rs2_step, 1)
                g.wait_ge(rs2_step, s + 4)
                settled(g)
                g.tensor_scalar(rs2[:, 4, :], rs2[:, 3, :], 0.0, EPS, ALU.max, ALU.add).then_inc(rs2_step, 1)
                g.wait_ge(rs2_step, s + 5)
                g.tensor_tensor(rs2[:, 5, :], rs2[:, 4, :], nhalf[:], ALU.pow).then_inc(rs2_step, 1)
                g.wait_ge(rs2_step, s + 6)
                settled(g)
                g.tensor_scalar(rs2[:, 6, :], rs2[:, 5, :], wmean[:, 1:2], 0.0, ALU.mult, ALU.add).then_inc(rs2_done, 1)

            def rs_ln3(i):
                g.wait_ge(mv3_done, i + 1)
                if later(i):
                    g.wait_ge(fin_done, i)
                settled(g)
                g.tensor_scalar(rs3[:, 0, :], mv3[:, :, 1], EPS, 1.0, ALU.add, ALU.mult).then_inc(rs3_step, 1)
                g.wait_ge(rs3_step, i + 1)
                g.tensor_tensor(rs3[:, 1, :], rs3[:, 0, :], nhalf[:], ALU.pow).then_inc(rs3_done, 1)

            def step(i, j):
                if here(i - 3):
                    for stage in range(3):
                        fold(i - 3, stage)
                if here(i + 1):
                    keeps(i + 1, (j + 1) % JT, 0, 2 if later(i) else 6)
                if here(i - 3):
                    rs_ln2(i - 3)
                if here(i):
                    beta_arg(i, 0)
                    beta_arg(i, 1)
                if here(i - 1):
                    rs_ln1(i - 1)
                if here(i):
                    gamma_arg(i, 0)
                    gamma_arg(i, 1)
                if here(i + 1) and later(i):
                    keeps(i + 1, (j + 1) % JT, 2, 6)
                if here(i - 3):
                    rs_ln3(i - 3)
                if here(i):
                    other_beta(i, 0)
                    other_beta(i, 1)
                if here(i - 1):
                    if isinstance(i, int) and i == 1:
                        g.wait_ge(w_done, 1)
                    add_const(i - 1, (j - 1) % JT)

            keeps(0, 0, 0, 6)
            steps(step, g)


_INS = ["hidden", "Wk", "Wv", "Wr", "Wo", "time_decay", "time_first", "time_mix_key", "time_mix_value",
        "time_mix_receptance"]
_FFN = ["ln1_g", "ln1_b", "w1", "b1", "ln2_g", "ln2_b", "w2", "b2"]


def kernel(**inputs):
    import concourse.bacc as bacc
    from concourse.bass_utils import run_bass_kernel_spmd

    nc = bacc.Bacc("TRN2", target_bir_lowering=False, num_devices=1)
    names = [f"L0_attn_{n}" for n in _INS] + [f"L0_ffn_{n}" for n in _FFN]
    laid = {name: inputs[name] for name in names}
    for name in laid:
        a = np.asarray(laid[name])
        if name.endswith(("_w1", "_w2")):
            laid[name] = a.T
        elif a.ndim == 1 and not name.endswith("_b2"):
            laid[name] = a.reshape(-1, P).T
    hidden = laid.pop("L0_attn_hidden")
    laid = {"hidden": hidden, "hidden_by_channel": np.transpose(np.asarray(hidden), (0, 2, 1)), **laid}
    arrays, args = {}, []
    for name, a in laid.items():
        a = np.ascontiguousarray(a)
        arrays[f"in_{name}"] = a
        args.append(nc.dram_tensor(f"in_{name}", a.shape, mybir.dt.from_np(a.dtype), kind="ExternalInput").ap())
    shape = inputs["L0_attn_hidden"].shape
    args.append(nc.dram_tensor("out", shape, F32, kind="ExternalOutput").ap())
    build(nc, *args)
    return run_bass_kernel_spmd(nc, [arrays], core_ids=[0]).results[0]["out"]
```

```python
from contextlib import ExitStack

import numpy as np

import concourse.bass as bass
from concourse import mybir

F32 = mybir.dt.float32
BF16 = mybir.dt.bfloat16
F16 = mybir.dt.float16
ALU = mybir.AluOpType
ACT = mybir.ActivationFunctionType
AX = mybir.AxisListType

P = 128
TOK = 512
Q = TOK // P
EPS = 1e-5
UP = 3
KEEPS = 4
NO_MAX = -1e38


def build(nc, x_in, x_by_channel, Wk, Wv, Wr, Wo, time_decay, time_first, mix_k, mix_v, mix_r,
          ln1_g, ln1_b, w1, b1, ln2_g, ln2_b, w2, b2, out):
    B, T, H = x_in.shape
    F = w1.shape[1]
    KC = H // P
    FC = F // P
    JT = T // TOK
    NT = B * JT
    assert H == KC * P and KC == 2 and F == FC * P and T == JT * TOK and Q == 4 and JT == 4

    x_rows = x_in.rearrange("b (j q p) h -> (b j) p q h", q=Q, p=P)
    x_cols = x_by_channel.rearrange("b (c p) t -> p b c t", p=P)
    out_rows = out.rearrange("b (j q p) h -> (b j) p q h", q=Q, p=P)

    with ExitStack() as ctx:
        def sb(name, shape, dtype=F32):
            return ctx.enter_context(nc.sbuf_tensor(name, shape, dtype))

        def ps(name, shape):
            return ctx.enter_context(nc.psum_tensor(name, shape, F32))

        def sem(name):
            return ctx.enter_context(nc.semaphore(name))

        ident = sb("ident", [P, P])
        ones = sb("ones", [P, P])
        wkvr = sb("wkvr", [P, 3, KC, H])
        wo = sb("wo", [P, KC, H])
        w1_tern = sb("w1_tern", [P, KC, F], BF16)
        w2_hi = sb("w2_hi", [P, FC, H + 1], F16)
        w2_lo = sb("w2_lo", [P, FC, H], F16)
        tcol = sb("tcol", [P, 5, KC])
        ntd = sb("ntd", [P, KC])
        td = sb("td", [P, KC])
        htf = sb("htf", [P, KC])
        omix = sb("omix", [P, 3, KC])
        lncol = sb("lncol", [P, 2, KC])
        fcol = sb("fcol", [P, 3, FC])
        wabs = sb("wabs", [P, 2])
        wmean = sb("wmean", [P, 2])
        wscale = sb("wscale", [P, 2])
        const_row = sb("const_row", [P, H])
        init = sb("init", [P, 4])
        nhalf = sb("nhalf", [P, 2, Q])

        x_tok = sb("x_tok", [P, 4, Q, H])
        xT = sb("xT", [P, JT, KC, TOK + 1])
        keep = sb("keep", [P, KEEPS, TOK])
        mixed = sb("mixed", [P, 3, KC, TOK])
        hist = sb("hist", [P, KC, 4, TOK + 1])
        dlt = sb("dlt", [P, KC, TOK])
        e1 = sb("e1", [P, KC, TOK])
        e2 = sb("e2", [P, KC, TOK])
        m2 = sb("m2", [P, KC, TOK])
        beta = sb("beta", [P, KC, TOK])
        val = sb("val", [P, KC, TOK])
        tr = sb("tr", [P, KC, TOK])
        rwkv = sb("rwkv", [P, KC, TOK])
        hn = sb("hn", [P, Q, H])
        x1c = sb("x1c", [P, 4, Q, H])
        hT = sb("hT", [P, KC, TOK])
        hT_hi = sb("hT_hi", [P, KC, TOK], BF16)
        hT_lo = sb("hT_lo", [P, KC, TOK], F16)
        u = sb("u", [P, FC, TOK])
        u_hi = sb("u_hi", [P, FC, TOK], BF16)
        u_lo = sb("u_lo", [P, FC, TOK], F16)
        usq = sb("usq", [P, FC, TOK])
        proj = sb("proj", [P, Q, H + 1])
        sq_tok = sb("sq_tok", [P, Q])
        z_tok = sb("z_tok", [P, Q, H])
        bn1 = sb("bn1", [P, Q, 6])
        mv1 = sb("mv1", [P, Q, 2])
        rs1 = sb("rs1", [P, 4, Q])
        rs2 = sb("rs2", [P, 8, Q])
        bn3 = sb("bn3", [P, Q, 6])
        mv3 = sb("mv3", [P, Q, 2])
        rs3 = sb("rs3", [P, 4, Q])

        kvr_ps = ps("kvr_ps", [P, 3, 512])
        up_ps = ps("up_ps", [P, UP, 512])
        row_ps = ps("row_ps", [P, 2, 512])
        sum_ps = row_ps[:, 1, H + 1:H + 1 + Q]

        ld_w = sem("ld_w"); ld_wkvr = sem("ld_wkvr"); ld_w12 = sem("ld_w12"); ld_ffn = sem("ld_ffn")
        st_out = sem("st_out")
        ld_xT = [sem(f"ld_xT{j}") for j in range(JT)]
        ld_x = [sem(f"ld_x{j}") for j in range(JT)]
        s_passed = sem("s_passed"); s_ones = sem("s_ones"); s_ident = sem("s_ident"); s_init = sem("s_init")
        s_half = sem("s_half"); s_zero = sem("s_zero"); xt_first = sem("xt_first")
        w_cols = sem("w_cols"); w_ntd = sem("w_ntd"); w_abs = sem("w_abs"); w_sum = sem("w_sum")
        w_mean = sem("w_mean"); w_inv = sem("w_inv"); wo_done = sem("wo_done")
        w1_cut = sem("w1_cut"); w1_done = sem("w1_done")
        w2_cut = sem("w2_cut"); w2_tern_done = sem("w2_tern_done"); w2_scaled = sem("w2_scaled")
        w2_centred = sem("w2_centred"); w2_hi_done = sem("w2_hi_done"); w2_done = sem("w2_done")
        w2_ones = sem("w2_ones")
        bias_done = sem("bias_done"); rows_ready = sem("rows_ready"); mean_done = sem("mean_done")
        const_done = sem("const_done")
        kept = sem("kept"); mix_done = sem("mix_done")
        k_ready = sem("k_ready"); v_ready = sem("v_ready"); r_ready = sem("r_ready"); v_done = sem("v_done")
        tr_done = sem("tr_done")
        mx_done = sem("mx_done"); dlt_done = sem("dlt_done"); m_done = sem("m_done"); e_done = sem("e_done")
        den_done = sem("den_done"); ln_done = sem("ln_done")
        barg_done = sem("barg_done"); garg_done = sem("garg_done"); beta_done = sem("beta_done")
        obeta_done = sem("obeta_done"); bv_done = sem("bv_done"); gam_done = sem("gam_done")
        avg_done = sem("avg_done"); wdf_done = sem("wdf_done"); g1_done = sem("g1_done")
        o1_done = sem("o1_done"); rwkv_done = sem("rwkv_done"); carried = sem("carried")
        att_ready = sem("att_ready"); y_done = sem("y_done"); bn1_done = sem("bn1_done")
        mv1_done = sem("mv1_done"); rs1_step = sem("rs1_step"); rs1_done = sem("rs1_done")
        hn_done = sem("hn_done"); x1_done = sem("x1_done"); x1c_done = sem("x1c_done")
        ht_ready = sem("ht_ready"); ht_evac = sem("ht_evac"); split_hi = sem("split_hi")
        split_done = sem("split_done")
        up_ready = sem("up_ready"); u_done = sem("u_done"); hi_done = sem("hi_done")
        lo_a_done = sem("lo_a_done"); lo_b_done = sem("lo_b_done"); usq_done = sem("usq_done")
        folded = sem("folded"); sums_ready = sem("sums_ready"); sums_done = sem("sums_done")
        down_ready = sem("down_ready"); proj_done = sem("proj_done"); rs2_step = sem("rs2_step")
        rs2_done = sem("rs2_done")
        z_done = sem("z_done"); bn3_done = sem("bn3_done"); mv3_done = sem("mv3_done")
        rs3_step = sem("rs3_step"); rs3_done = sem("rs3_done"); fin_done = sem("fin_done")

        obeta, bv, wdf = m2, e1, e2
        flat_u, flat_usq = (a[:].rearrange("p c t -> p (c t)") for a in (u, usq))
        w1_raw, w1_pos = flat_u[:, 0:FC * H], flat_u[:, FC * H:2 * FC * H]
        w2_raw, w2_pos = flat_usq[:, 0:FC * H], flat_usq[:, FC * H:2 * FC * H]
        w2_tern, w2_full = (a[:].rearrange("p c t -> p (c t)").bitcast(F32).rearrange("p (c h) -> p c h", c=FC)
                            for a in (u_lo, u_hi))
        mean_row = z_tok[:, 0, :]
        bias_rows = x1c[:, 3].rearrange("p q h -> p (q h)").rearrange("p (c m) -> p c m", c=FC)

        def here(i):
            return not isinstance(i, int) or 0 <= i < NT

        def later(i):
            return not isinstance(i, int) or i > 0

        def rounds(i, j, each):
            return (i - j) // JT * each + each if isinstance(i, int) else (i - j) * (each // JT) + each

        def steps(run, eng):
            for i in range(JT + 1):
                run(i, i % JT)
            with eng.Fori(1, B - 1) as b:
                for j in range(1, JT + 1):
                    run(b * JT + j, j % JT)
            for i in range(NT - JT + 1, NT + 4):
                run(i, i % JT)

        block = ctx.enter_context(nc.Block())

        def settled(eng):
            eng.sem_inc(s_passed, 1)

        @block.sync
        def _(sp):
            def load_rows(i, j):
                sp.dma_start(x_tok[:, j], x_rows[i]).then_inc(ld_x[j], 16)

            def load_cols(j, b):
                for c in range(KC):
                    if j == 0:
                        sp.dma_start(xT[:, 0, c, 1:TOK + 1], x_cols[:, b, c, 0:TOK]).then_inc(ld_xT[0], 16)
                    else:
                        sp.dma_start(xT[:, j, c, :], x_cols[:, b, c, j * TOK - 1:(j + 1) * TOK]).then_inc(ld_xT[j], 16)

            load_cols(0, 0)
            for n, vec in enumerate((time_decay, time_first, mix_k, mix_v, mix_r)):
                sp.dma_start(tcol[:, n, :], vec).then_inc(ld_w, 16)
            for n, w in enumerate((Wk, Wv, Wr)):
                sp.dma_start(wkvr[:, n], w.rearrange("(c p) n -> p c n", p=P)).then_inc(ld_wkvr, 16)
            sp.dma_start(w1_raw.rearrange("p (c f) -> p c f", c=KC),
                         w1.rearrange("(c p) n -> p c n", p=P)).then_inc(ld_w12, 16)
            sp.dma_start(w2_raw.rearrange("p (c h) -> p c h", c=FC),
                         w2.rearrange("(c p) n -> p c n", p=P)).then_inc(ld_w12, 16)
            load_cols(1, 0)
            load_rows(0, 0)
            sp.dma_start(wo[:], Wo.rearrange("(c p) n -> p c n", p=P)).then_inc(ld_ffn, 16)
            for n, vec in enumerate((ln1_g, ln1_b)):
                sp.dma_start(lncol[:, n, :], vec).then_inc(ld_ffn, 16)
            for n, vec in enumerate((b1, ln2_g, ln2_b)):
                sp.dma_start(fcol[:, n, :], vec).then_inc(ld_ffn, 16)
            sp.dma_start(const_row[:], b2.partition_broadcast(P)).then_inc(ld_ffn, 16)
            load_rows(1, 1)
            for j in range(2, JT):
                load_cols(j, 0)
                load_rows(j, j)

            def step(i, j, b):
                if here(i + 3):
                    sp.wait_ge(x1_done, i)
                    settled(sp)
                    sp.wait_ge(mix_done, 6 * i)
                    settled(sp)
                    load_rows(i + 3, (j + 3) % JT)
                    load_cols((j + 3) % JT, b if j == 0 else b + 1)
                if here(i - 4):
                    sp.wait_ge(fin_done, i - 3)
                    settled(sp)
                    sp.dma_start(out_rows[i - 4], z_tok[:]).then_inc(st_out, 16)

            for i in range(1, JT + 1):
                step(i, i % JT, i // JT)
            with sp.Fori(1, B - 1) as b:
                for j in range(1, JT + 1):
                    step(b * JT + j, j % JT, b if j < JT else b + 1)
            for i in range(NT - JT + 1, NT + 4):
                step(i, i % JT, i // JT)
            sp.wait_ge(st_out, 16 * NT)

        @block.tensor
        def _(pe):
            def kvr(i):
                to_k, to_v, to_r = (0, dlt_done, k_ready), (1, v_done, v_ready), (2, tr_done, r_ready)
                for h in range(KC):
                    n = KC * i + h
                    for w, used, ready in ((to_k, to_v, to_r), (to_v, to_k, to_r))[h]:
                        if h == 0:
                            pe.wait_ge(mix_done, 6 * i + 2 * (w + 1))
                        if later(n):
                            pe.wait_ge(used, n)
                        for c in range(KC):
                            m = pe.matmul(kvr_ps[:, w, :], wkvr[:, w, c, h * P:(h + 1) * P],
                                          mixed[:, w, c, :], start=(c == 0), stop=(c == KC - 1))
                        m.then_inc(ready, 1)

            def turn_h(i):
                pe.wait_ge(hn_done, i + 1)
                if later(i):
                    pe.wait_ge(u_done, FC * i)
                for c in range(KC):
                    for q in range(Q):
                        m = pe.transpose(up_ps[:, c, q * P:(q + 1) * P], hn[:, q, c * P:(c + 1) * P], ident[:])
                    m.then_inc(ht_ready, 1)

            def att(i):
                pe.wait_ge(rwkv_done, KC * (i + 1))
                if later(i - 2):
                    pe.wait_ge(proj_done, Q * (i - 2))
                for g in range(2):
                    for q in range(2):
                        t = slice((2 * g + q) * P, (2 * g + q + 1) * P)
                        for c in range(KC):
                            m = pe.matmul(row_ps[:, g, q * H:(q + 1) * H], rwkv[:, c, t], wo[:, c, :],
                                          start=(c == 0), stop=(c == KC - 1))
                    m.then_inc(att_ready, 1)

            def sums(i):
                pe.wait_ge(folded, 3 * i + 3)
                if here(i + 2):
                    pe.wait_ge(y_done, 2 * (i + 3))
                else:
                    pe.wait_ge(proj_done, Q * i)
                for q in range(Q):
                    m = pe.matmul(sum_ps[:, q:q + 1], usq[:, 0, q * P:(q + 1) * P], ones[:, 0:1],
                                  start=True, stop=True)
                m.then_inc(sums_ready, 1)

            def up(i, between):
                for f in range(FC):
                    if f == UP and between:
                        sums(i - 1)
                    if f >= UP:
                        pe.wait_ge(u_done, FC * i + f - UP + 1)
                    if isinstance(i, int) and i == 0 and f == 2:
                        pe.wait_ge(const_done, 1)
                    for c in range(KC):
                        if f == 0:
                            pe.wait_ge(split_done, KC * i + c + 1)
                        pe.matmul(up_ps[:, f % UP, :], w1_tern[:, c, f * P:(f + 1) * P], hT_hi[:, c, :],
                                  start=(c == 0), stop=False)
                        m = pe.matmul(up_ps[:, f % UP, :], w1_tern[:, c, f * P:(f + 1) * P], hT_lo[:, c, :],
                                      start=False, stop=(c == KC - 1))
                    m.then_inc(up_ready, 1)

            def down(i):
                if here(i + 2):
                    pe.wait_ge(y_done, 2 * (i + 3))
                for q in range(Q):
                    t = slice(q * P, (q + 1) * P)
                    if q >= 2 or not here(i + 2):
                        pe.wait_ge(proj_done, Q * i + q - 1)
                    if q == 1:
                        pe.wait_ge(sums_done, i + 1)
                    for f in range(FC):
                        if q == 0 and f == 0:
                            pe.wait_ge(lo_a_done, i + 1)
                        if q == 0 and f == FC // 2:
                            pe.wait_ge(lo_b_done, i + 1)
                        pe.matmul(row_ps[:, q % 2, 0:H + 1], u_hi[:, f, t], w2_hi[:, f, :],
                                  start=(f == 0), stop=False)
                        pe.matmul(row_ps[:, q % 2, 0:H], u_hi[:, f, t], w2_lo[:, f, :],
                                  start=False, stop=False)
                        m = pe.matmul(row_ps[:, q % 2, 0:H + 1], u_lo[:, f, t], w2_hi[:, f, :],
                                      start=False, stop=(f == FC - 1))
                    m.then_inc(down_ready, 1)

            def weight_sums():
                pe.wait_ge(s_ones, 1)
                pe.wait_ge(w_abs, 2)
                pe.matmul(row_ps[:, 0, 0:2], ones[:], wabs[:], start=True, stop=True).then_inc(w_sum, 1)

            def weight_rows():
                pe.wait_ge(w2_tern_done, 1)
                pe.wait_ge(bias_done, 1)
                pe.wait_ge(w2_scaled, 1)
                for f in range(FC):
                    pe.matmul(up_ps[:, 2, 0:H], bias_rows[:, f, :], w2_tern[:, f, :],
                              start=(f == 0), stop=(f == FC - 1))
                for f in range(FC):
                    m = pe.matmul(up_ps[:, 2, H:2 * H], ones[:], w2_full[:, f, :],
                                  start=(f == 0), stop=(f == FC - 1))
                m.then_inc(rows_ready, 1)

            def step(i, j):
                if here(i):
                    kvr(i)
                if isinstance(i, int) and i == 0:
                    weight_sums()
                if here(i - 2):
                    if isinstance(i, int) and i == 2:
                        pe.wait_ge(s_ident, 1)
                    turn_h(i - 2)
                if here(i - 1):
                    if isinstance(i, int) and i == 1:
                        pe.wait_ge(wo_done, 1)
                        pe.wait_ge(w_mean, 1)
                    att(i - 1)
                if isinstance(i, int) and i == 2:
                    weight_rows()
                    pe.wait_ge(w1_done, 1)
                if here(i - 2):
                    up(i - 2, here(i - 3))
                if here(i - 3) and not here(i - 2):
                    sums(i - 3)
                if here(i - 3):
                    if isinstance(i, int) and i == 3:
                        pe.wait_ge(w2_ones, 1)
                        pe.wait_ge(w2_done, 1)
                    down(i - 3)

            pe.wait_ge(ld_wkvr, 48)
            steps(step, pe)

        @block.scalar
        def _(act):
            def wkv_weights(i, h):
                n = KC * i + h
                act.wait_ge(v_ready, n + 1)
                if later(i):
                    act.wait_ge(rwkv_done, n - 1)
                act.activation(val[:, h, :], kvr_ps[:, 1, :], ACT.Copy).then_inc(v_done, 1)
                act.wait_ge(r_ready, n + 1)
                act.activation(tr[:, h, :], kvr_ps[:, 2, :], ACT.Tanh, scale=0.5).then_inc(tr_done, 1)
                act.wait_ge(m_done, 2 * n + 1)
                act.activation(e1[:, h, :], e1[:, h, :], ACT.Exp, bias=td[:, h:h + 1], scale=-1.0).then_inc(e_done, 1)
                act.wait_ge(m_done, 2 * n + 2)
                act.activation(e2[:, h, :], m2[:, h, :], ACT.Exp, bias=ntd[:, h:h + 1]).then_inc(e_done, 1)

            def split_u(i, part):
                f = slice(part * FC // 2, (part + 1) * FC // 2)
                if later(i):
                    act.wait_ge(down_ready, Q * i)
                act.wait_ge(u_done, FC * (i + 1))
                act.activation(u_hi[:, f, :], u[:, f, :], ACT.Copy).then_inc(hi_done, 1)

            def evac_h(i):
                if later(i):
                    act.wait_ge(split_done, KC * i)
                for c in range(KC):
                    act.wait_ge(ht_ready, KC * i + c + 1)
                    act.activation(hT[:, c, :], up_ps[:, c, :], ACT.Identity, bias=lncol[:, 1, c:c + 1],
                                   scale=lncol[:, 0, c:c + 1]).then_inc(ht_evac, 1)

            def ln_den(i):
                for h in range(KC):
                    act.wait_ge(den_done, KC * i + h + 1)
                    act.activation(hist[:, h, 1, 1:TOK + 1], hist[:, h, 3, 1:TOK + 1], ACT.Ln).then_inc(ln_done, 1)

            def copy_sums(i):
                act.wait_ge(sums_ready, i + 1)
                if later(i):
                    act.wait_ge(rs2_done, i)
                act.activation(sq_tok[:], sum_ps[:, 0:Q], ACT.Copy).then_inc(sums_done, 1)

            def gelus(i):
                for f in range(FC):
                    if later(i) and f == 0:
                        act.wait_ge(lo_a_done, i)
                    if later(i) and f == FC // 2:
                        act.wait_ge(lo_b_done, i)
                    act.wait_ge(up_ready, FC * i + f + 1)
                    act.activation(u[:, f, :], up_ps[:, f % UP, :], ACT.Gelu, bias=fcol[:, 0, f:f + 1],
                                   scale=wmean[:, 0:1]).then_inc(u_done, 1)

            def betas(i):
                for h in range(KC):
                    n = KC * i + h
                    act.wait_ge(barg_done, n + 1)
                    act.activation(beta[:, h, :], beta[:, h, :], ACT.Exp, bias=ntd[:, h:h + 1]).then_inc(beta_done, 1)
                    act.wait_ge(beta_done, n + 1)
                    act.activation(obeta[:, h, :], beta[:, h, :], ACT.Identity, bias=ones[:, 0:1],
                                   scale=-1.0).then_inc(obeta_done, 1)

            def gammas(i):
                for h in range(KC):
                    n = KC * i + h
                    act.wait_ge(garg_done, n + 1)
                    act.activation(dlt[:, h, :], dlt[:, h, :], ACT.Tanh, bias=htf[:, h:h + 1],
                                   scale=0.5).then_inc(gam_done, 1)

            def copy_down(i, q):
                if later(i):
                    act.wait_ge(z_done, Q * i)
                act.wait_ge(down_ready, Q * i + q + 1)
                act.activation(proj[:, q, :], row_ps[:, q % 2, 0:H + 1], ACT.Copy).then_inc(proj_done, 1)

            def squares(i, part):
                f = slice(part * FC // 2, (part + 1) * FC // 2)
                if later(i):
                    act.wait_ge(sums_ready, i)
                act.wait_ge(u_done, FC * (i + 1))
                act.activation(usq[:, f, :], u[:, f, :], ACT.Square).then_inc(usq_done, 1)

            def z_end(i):
                act.wait_ge(rs3_done, i + 1)
                for q in range(Q):
                    m = act.activation(z_tok[:, q, :], z_tok[:, q, :], ACT.Identity, bias=rs3[:, 3, q:q + 1],
                                       scale=rs3[:, 1, q:q + 1])
                m.then_inc(fin_done, 1)

            def weight_abs():
                act.wait_ge(ld_w12, 16 * 2)
                act.activation(w1_pos, w1_raw, ACT.Abs, accum_out=wabs[:, 0:1]).then_inc(w_abs, 1)
                act.activation(w2_pos, w2_raw, ACT.Abs, accum_out=wabs[:, 1:2]).then_inc(w_abs, 1)
                act.wait_ge(ld_ffn, 16 * 7)
                act.activation(wo[:], wo[:], ACT.Copy, scale=0.5).then_inc(wo_done, 1)

            def weight_scales():
                act.wait_ge(s_ones, 1)
                for f in range(FC):
                    m = act.activation(bias_rows[:, f, :], ones[:], ACT.Copy, scale=fcol[:, 2, f:f + 1])
                m.then_inc(bias_done, 1)
                act.wait_ge(w2_tern_done, 1)
                for f in range(FC):
                    m = act.activation(w2_full[:, f, :], w2_tern[:, f, :], ACT.Copy, scale=fcol[:, 1, f:f + 1])
                m.then_inc(w2_scaled, 1)

            def step(i, j):
                early = isinstance(i, int) and i < 3
                if here(i - 2) and not here(i):
                    evac_h(i - 2)
                if here(i - 3) and not (isinstance(i, int) and i == 3):
                    split_u(i - 3, 0)
                if here(i):
                    wkv_weights(i, 0)
                if isinstance(i, int) and i == 3:
                    act.wait_ge(w2_done, 1)
                    split_u(i - 3, 0)
                if isinstance(i, int) and i == 0:
                    weight_abs()
                if here(i - 3):
                    split_u(i - 3, 1)
                if here(i):
                    wkv_weights(i, 1)
                if here(i - 2) and here(i):
                    evac_h(i - 2)
                if here(i):
                    ln_den(i)
                if early:
                    betas(i)
                    gammas(i)
                if here(i - 2):
                    if isinstance(i, int) and i == 2:
                        act.wait_ge(w1_done, 1)
                    gelus(i - 2)
                if here(i - 3):
                    copy_sums(i - 3)
                if here(i - 2) and not here(i):
                    squares(i - 2, 0)
                if here(i) and not early:
                    betas(i)
                if here(i - 3):
                    copy_down(i - 3, 0)
                if here(i) and not early:
                    gammas(i)
                if isinstance(i, int) and i == 1:
                    weight_scales()
                if isinstance(i, int) and i == 2:
                    act.wait_ge(w2_centred, 1)
                    act.activation(w2_hi[:, :, 0:H], w2_full, ACT.Copy).then_inc(w2_hi_done, 1)
                if here(i - 2) and not here(i):
                    squares(i - 2, 1)
                if here(i - 3):
                    copy_down(i - 3, 1)
                if here(i - 2) and here(i):
                    squares(i - 2, 0)
                if here(i - 3):
                    copy_down(i - 3, 2)
                if here(i - 4):
                    z_end(i - 4)
                if here(i - 3):
                    copy_down(i - 3, 3)
                if here(i - 2) and here(i):
                    squares(i - 2, 1)

            act.wait_ge(ld_w, 16 * 5)
            act.activation(ntd[:], tcol[:, 0, :], ACT.Exp).then_inc(w_ntd, 1)
            act.wait_ge(w_cols, 3)
            steps(step, act)

        @block.vector
        def _(v):
            def wkv_a(i, h):
                n = KC * i + h
                k = kvr_ps[:, 0, :]
                d = dlt[:, h, :]
                v.wait_ge(k_ready, n + 1)
                v.wait_ge(carried, n + 1)
                v.tensor_tensor_scan(hist[:, h, 0, 1:TOK + 1], td[:, h:h + 1].broadcast_to([P, TOK]), k,
                                     hist[:, h, 0, 0:1], ALU.add, ALU.max).then_inc(mx_done, 1)
                v.wait_ge(mx_done, n + 1)
                v.tensor_tensor(d, k, hist[:, h, 0, 0:TOK], ALU.subtract).then_inc(dlt_done, 1)
                v.wait_ge(dlt_done, n + 1)
                v.tensor_scalar(e1[:, h, :], d, td[:, h:h + 1], None, ALU.max).then_inc(m_done, 1)
                v.tensor_scalar(m2[:, h, :], d, td[:, h:h + 1], None, ALU.min).then_inc(m_done, 1)

            def wkv_b(i, h):
                n = KC * i + h
                v.wait_ge(e_done, 2 * n + 2)
                v.tensor_tensor_scan(hist[:, h, 3, 1:TOK + 1], e1[:, h, :], e2[:, h, :],
                                     hist[:, h, 3, 0:1], ALU.mult, ALU.add).then_inc(den_done, 1)

            def wkv_c(i, j):
                for h in range(KC):
                    n = KC * i + h
                    v.wait_ge(v_done, n + 1)
                    v.wait_ge(beta_done, n + 1)
                    v.tensor_tensor(bv[:, h, :], val[:, h, :], beta[:, h, :], ALU.mult).then_inc(bv_done, 1)
                for h in range(KC):
                    n = KC * i + h
                    v.wait_ge(bv_done, n + 1)
                    v.wait_ge(obeta_done, n + 1)
                    v.tensor_tensor_scan(hist[:, h, 2, 1:TOK + 1], obeta[:, h, :], bv[:, h, :],
                                         hist[:, h, 2, 0:1], ALU.mult, ALU.add).then_inc(avg_done, 1)
                for h in range(KC):
                    n = KC * i + h
                    v.wait_ge(avg_done, n + 1)
                    v.tensor_tensor(wdf[:, h, :], val[:, h, :], hist[:, h, 2, 0:TOK], ALU.subtract).then_inc(wdf_done, 1)
                for h in range(KC):
                    n = KC * i + h
                    v.wait_ge(wdf_done, n + 1)
                    v.wait_ge(gam_done, n + 1)
                    v.scalar_tensor_tensor(out=wdf[:, h, :], in0=dlt[:, h, :], scalar=1.0, in1=wdf[:, h, :],
                                           op0=ALU.add, op1=ALU.mult).then_inc(g1_done, 1)
                for h in range(KC):
                    n = KC * i + h
                    v.wait_ge(g1_done, n + 1)
                    v.scalar_tensor_tensor(out=wdf[:, h, :], in0=wdf[:, h, :], scalar=0.5, in1=hist[:, h, 2, 0:TOK],
                                           op0=ALU.mult, op1=ALU.add).then_inc(o1_done, 1)
                for h in range(KC):
                    n = KC * i + h
                    v.wait_ge(o1_done, n + 1)
                    v.wait_ge(tr_done, n + 1)
                    if later(i):
                        v.wait_ge(att_ready, 2 * i)
                    v.scalar_tensor_tensor(out=rwkv[:, h, :], in0=tr[:, h, :], scalar=1.0, in1=wdf[:, h, :],
                                           op0=ALU.add, op1=ALU.mult).then_inc(rwkv_done, 1)
                    v.wait_ge(garg_done, n + 1)
                    src = init[:] if j == JT - 1 else hist[:, h, :, TOK]
                    v.tensor_copy(hist[:, h, :, 0], src).then_inc(carried, 1)

            def lo_u(i, part, done):
                f = slice(part * FC // 2, (part + 1) * FC // 2)
                v.wait_ge(hi_done, 2 * i + part + 1)
                v.tensor_tensor(u_lo[:, f, :], u[:, f, :], u_hi[:, f, :], ALU.subtract).then_inc(done, 1)

            def mix(i, j):
                rot = 2 * (j % 2)
                if later(i):
                    v.wait_ge(r_ready, KC * i)
                for n in range(6):
                    w, c = n // KC, n % KC
                    v.wait_ge(kept, 6 * i + n + 1)
                    v.scalar_tensor_tensor(out=mixed[:, w, c, :], in0=xT[:, j, c, 1:TOK + 1],
                                           scalar=tcol[:, 2 + w, c:c + 1], in1=keep[:, (n + rot) % KEEPS, :],
                                           op0=ALU.mult, op1=ALU.add).then_inc(mix_done, 1)

            def split_h(i):
                if later(i):
                    v.wait_ge(up_ready, FC * i)
                for c in range(KC):
                    v.wait_ge(ht_evac, KC * i + c + 1)
                    v.tensor_copy(hT_hi[:, c, :], hT[:, c, :]).then_inc(split_hi, 1)
                    v.wait_ge(split_hi, KC * i + c + 1)
                    v.tensor_tensor(hT_lo[:, c, :], hT[:, c, :], hT_hi[:, c, :], ALU.subtract).then_inc(split_done, 1)

            def residual(i, j):
                v.wait_ge(ld_x[j], rounds(i, j, 16))
                y = x_tok[:, j].rearrange("p (g q) h -> p g (q h)", g=2)
                for g in range(2):
                    v.wait_ge(att_ready, 2 * i + g + 1)
                    v.tensor_tensor(y[:, g], row_ps[:, g, :], y[:, g], ALU.add).then_inc(y_done, 1)
                for q in range(Q):
                    v.wait_ge(y_done, 2 * i + q // 2 + 1)
                    m = v.bn_stats(bn1[:, q, :], x_tok[:, j, q, :])
                m.then_inc(bn1_done, 1)
                v.wait_ge(bn1_done, i + 1)
                settled(v)
                for q in range(Q):
                    m = v.bn_aggr(mv1[:, q, :], bn1[:, q, :])
                m.then_inc(mv1_done, 1)

            def norm1(i, j):
                v.wait_ge(mv1_done, i + 1)
                v.wait_ge(rs1_done, i + 1)
                if later(i):
                    v.wait_ge(ht_ready, KC * i)
                for q in range(Q):
                    m = v.tensor_scalar(hn[:, q, :], x_tok[:, j, q, :], mv1[:, q, 0:1], rs1[:, 3, q:q + 1],
                                        ALU.subtract, ALU.mult)
                m.then_inc(hn_done, 1)
                for q in range(Q):
                    m = v.tensor_scalar(x1c[:, j, q, :], x_tok[:, j, q, :], mv1[:, q, 0:1], rs1[:, 2, q:q + 1],
                                        ALU.subtract, ALU.mult)
                m.then_inc(x1_done, 1)

            def z_part(i, j):
                if later(i):
                    v.wait_ge(st_out, 16 * i)
                v.wait_ge(x1c_done, i + 1)
                v.wait_ge(rs2_done, i + 1)
                for q in range(Q):
                    v.scalar_tensor_tensor(out=z_tok[:, q, :], in0=proj[:, q, 0:H], scalar=rs2[:, 6, q:q + 1],
                                           in1=x1c[:, j, q, :], op0=ALU.mult, op1=ALU.add).then_inc(z_done, 1)
                for q in range(Q):
                    v.wait_ge(z_done, Q * i + q + 1)
                    m = v.bn_stats(bn3[:, q, :], z_tok[:, q, :])
                m.then_inc(bn3_done, 1)
                v.wait_ge(bn3_done, i + 1)
                settled(v)
                for q in range(Q):
                    m = v.bn_aggr(mv3[:, q, :], bn3[:, q, :])
                m.then_inc(mv3_done, 1)

            def cut(raw, pos, n, done):
                v.tensor_scalar(pos, raw, wscale[:, n:n + 1], 0.5, ALU.mult, ALU.is_gt).then_inc(done, 1)
                v.tensor_scalar(raw, raw, wscale[:, n:n + 1], -0.5, ALU.mult, ALU.is_lt).then_inc(done, 1)

            def weight_means():
                v.wait_ge(w_sum, 1)
                v.tensor_scalar(wmean[:], row_ps[:, 0, 0:2], 1.0 / (F * H), 1e-5, ALU.mult, ALU.max).then_inc(w_mean, 1)
                v.wait_ge(w_mean, 1)
                v.reciprocal(wscale[:], wmean[:]).then_inc(w_inv, 1)
                v.wait_ge(w_inv, 1)
                v.wait_ge(w_abs, 2)

            def ternary_w1():
                v.wait_ge(w1_cut, 2)
                v.tensor_tensor(w1_tern[:].rearrange("p c f -> p (c f)"), w1_pos, w1_raw, ALU.subtract).then_inc(w1_done, 1)

            def row_constants():
                v.wait_ge(rows_ready, 1)
                v.tensor_scalar(mean_row, up_ps[:, 2, H:2 * H], 1.0 / F, None, ALU.mult).then_inc(mean_done, 1)
                v.wait_ge(ld_ffn, 16 * 7)
                v.scalar_tensor_tensor(out=const_row[:], in0=up_ps[:, 2, 0:H], scalar=wmean[:, 1:2], in1=const_row[:],
                                       op0=ALU.mult, op1=ALU.add).then_inc(const_done, 1)

            def step(i, j):
                early = isinstance(i, int) and i < 3
                if here(i):
                    wkv_a(i, 0)
                if isinstance(i, int) and i == 1:
                    cut(w1_raw, w1_pos, 0, w1_cut)
                if isinstance(i, int) and i == 2:
                    ternary_w1()
                if isinstance(i, int) and i == 3:
                    v.wait_ge(w2_hi_done, 1)
                    v.tensor_tensor(w2_lo[:], w2_full, w2_hi[:, :, 0:H], ALU.subtract).then_inc(w2_done, 1)
                if here(i - 2) and not here(i):
                    split_h(i - 2)
                if here(i - 3):
                    lo_u(i - 3, 0, lo_a_done)
                if here(i):
                    wkv_a(i, 1)
                    wkv_b(i, 0)
                    wkv_b(i, 1)
                if early:
                    mix(i + 1, (j + 1) % JT)
                if isinstance(i, int) and i == 0:
                    weight_means()
                    cut(w2_raw, w2_pos, 1, w2_cut)
                if here(i - 2) and here(i):
                    split_h(i - 2)
                if here(i - 3) and not here(i - 1):
                    lo_u(i - 3, 1, lo_b_done)
                if here(i - 1):
                    residual(i - 1, (j - 1) % JT)
                if here(i - 4):
                    z_part(i - 4, j)
                if isinstance(i, int) and i == 2:
                    row_constants()
                if early:
                    wkv_c(i, j)
                if here(i - 1):
                    norm1(i - 1, (j - 1) % JT)
                if here(i + 1) and not early:
                    mix(i + 1, (j + 1) % JT)
                if here(i) and not early:
                    wkv_c(i, j)

            v.wait_ge(ld_w, 16 * 5)
            v.tensor_scalar(omix[:], tcol[:, 2:5, :], -1.0, 1.0, ALU.mult, ALU.add).then_inc(w_cols, 1)
            v.tensor_scalar(htf[:], tcol[:, 1, :], 0.5, None, ALU.mult).then_inc(w_cols, 1)
            v.wait_ge(w_ntd, 1)
            v.tensor_scalar(td[:], ntd[:], -1.0, None, ALU.mult).then_inc(w_cols, 1)
            v.wait_ge(s_init, 2)
            for h in range(KC):
                v.tensor_copy(hist[:, h, :, 0], init[:]).then_inc(carried, 1)
            v.wait_ge(w_cols, 3)
            v.wait_ge(carried, 2)
            mix(0, 0)
            steps(step, v)

        @block.gpsimd
        def _(g):
            g.memset(xT[:, 0, :, 0:1], 0.0).then_inc(xt_first, 1)
            g.memset(init[:, 1:4], 0.0).then_inc(s_init, 1)
            g.memset(init[:, 0:1], NO_MAX).then_inc(s_init, 1)
            g.memset(ones[:], 1.0).then_inc(s_ones, 1)
            g.memset(nhalf[:], -0.5).then_inc(s_half, 1)
            g.memset(ident[:], 0.0).then_inc(s_zero, 1)
            g.memset(w2_hi[:, :, H:H + 1], 1.0).then_inc(w2_ones, 1)
            g.wait_ge(s_zero, 1)
            g.affine_select(out=ident[:], in_=ident[:], compare_op=ALU.not_equal, fill=1.0, base=0,
                            pattern=[[-1, P]], channel_multiplier=1).then_inc(s_ident, 1)
            g.wait_ge(s_half, 1)
            g.wait_ge(xt_first, 1)
            g.wait_ge(w_cols, 3)

            def fold(i, stage):
                half = FC >> (stage + 1)
                if stage == 0:
                    g.wait_ge(usq_done, 2 * (i + 1))
                else:
                    g.wait_ge(folded, 3 * i + stage)
                g.tensor_tensor(usq[:, 0:half, :], usq[:, 0:half, :], usq[:, half:2 * half, :], ALU.add).then_inc(folded, 1)

            def keeps(i, j, n0, n1):
                rot = 2 * (j % 2)
                g.wait_ge(ld_xT[j], rounds(i, j, 32))
                for n in range(n0, n1):
                    w, c = n // KC, n % KC
                    if later(i) or n >= KEEPS:
                        g.wait_ge(mix_done, 6 * i + n + 1 - KEEPS)
                    settled(g)
                    g.tensor_scalar(keep[:, (n + rot) % KEEPS, :], xT[:, j, c, 0:TOK], omix[:, w, c:c + 1], 0.0,
                                    ALU.mult, ALU.add).then_inc(kept, 1)

            def beta_arg(i, h):
                n = KC * i + h
                g.wait_ge(ln_done, n + 1)
                g.tensor_tensor(beta[:, h, :], m2[:, h, :], hist[:, h, 1, 1:TOK + 1], ALU.subtract).then_inc(barg_done, 1)

            def gamma_arg(i, h):
                n = KC * i + h
                g.wait_ge(m_done, 2 * n + 2)
                g.tensor_tensor(dlt[:, h, :], dlt[:, h, :], hist[:, h, 1, 0:TOK], ALU.subtract).then_inc(garg_done, 1)

            def lo_u(i):
                f = slice(FC // 2, FC)
                g.wait_ge(hi_done, 2 * i + 2)
                g.tensor_tensor(u_lo[:, f, :], u[:, f, :], u_hi[:, f, :], ALU.subtract).then_inc(lo_b_done, 1)

            def rs_ln1(i):
                g.wait_ge(mv1_done, i + 1)
                if later(i):
                    g.wait_ge(x1_done, i)
                settled(g)
                g.tensor_scalar(rs1[:, 0, :], mv1[:, :, 1], EPS, 1.0, ALU.add, ALU.mult).then_inc(rs1_step, 1)
                g.tensor_scalar(rs1[:, 1, :], mv1[:, :, 1], 1.0 + EPS, EPS * EPS, ALU.mult, ALU.add).then_inc(rs1_step, 1)
                g.wait_ge(rs1_step, 2 * i + 2)
                g.tensor_tensor(rs1[:, 2:4, :], rs1[:, 0:2, :], nhalf[:], ALU.pow).then_inc(rs1_done, 1)

            def add_const(i, j):
                g.wait_ge(x1_done, i + 1)
                for q in range(Q):
                    m = g.tensor_tensor(x1c[:, j, q, :], x1c[:, j, q, :], const_row[:], ALU.add)
                m.then_inc(x1c_done, 1)

            def rs_ln2(i):
                g.wait_ge(proj_done, Q * (i + 1))
                g.wait_ge(sums_done, i + 1)
                if later(i):
                    g.wait_ge(z_done, Q * i)
                s = 6 * i
                settled(g)
                g.tensor_scalar(rs2[:, 0, :], proj[:, :, H], 1.0 / F, 0.0, ALU.mult, ALU.add).then_inc(rs2_step, 1)
                g.tensor_scalar(rs2[:, 1, :], sq_tok[:], 1.0 / F, 0.0, ALU.mult, ALU.add).then_inc(rs2_step, 1)
                g.wait_ge(rs2_step, s + 2)
                g.tensor_tensor(rs2[:, 2, :], rs2[:, 0, :], rs2[:, 0, :], ALU.mult).then_inc(rs2_step, 1)
                g.wait_ge(rs2_step, s + 3)
                g.tensor_tensor(rs2[:, 3, :], rs2[:, 1, :], rs2[:, 2, :], ALU.subtract).then_inc(rs2_step, 1)
                g.wait_ge(rs2_step, s + 4)
                settled(g)
                g.tensor_scalar(rs2[:, 4, :], rs2[:, 3, :], 0.0, EPS, ALU.max, ALU.add).then_inc(rs2_step, 1)
                g.wait_ge(rs2_step, s + 5)
                g.tensor_tensor(rs2[:, 5, :], rs2[:, 4, :], nhalf[:, 0, :], ALU.pow).then_inc(rs2_step, 1)
                g.wait_ge(rs2_step, s + 6)
                settled(g)
                g.tensor_scalar(rs2[:, 6, :], rs2[:, 5, :], wmean[:, 1:2], 0.0, ALU.mult, ALU.add).then_inc(rs2_done, 1)

            def rs_ln3(i):
                g.wait_ge(mv3_done, i + 1)
                if later(i):
                    g.wait_ge(fin_done, i)
                settled(g)
                g.tensor_scalar(rs3[:, 0, :], mv3[:, :, 1], EPS, 1.0, ALU.add, ALU.mult).then_inc(rs3_step, 1)
                g.tensor_scalar(rs3[:, 2, :], mv3[:, :, 0], -1.0, 0.0, ALU.mult, ALU.add).then_inc(rs3_step, 1)
                g.wait_ge(rs3_step, 3 * i + 2)
                g.tensor_tensor(rs3[:, 1, :], rs3[:, 0, :], nhalf[:, 0, :], ALU.pow).then_inc(rs3_step, 1)
                g.wait_ge(rs3_step, 3 * i + 3)
                g.tensor_tensor(rs3[:, 3, :], rs3[:, 2, :], rs3[:, 1, :], ALU.mult).then_inc(rs3_done, 1)

            def ternary_w2():
                g.wait_ge(w2_cut, 2)
                g.tensor_tensor(w2_tern, w2_pos.rearrange("p (c h) -> p c h", c=FC),
                                w2_raw.rearrange("p (c h) -> p c h", c=FC), ALU.subtract).then_inc(w2_tern_done, 1)

            def centre_w2():
                g.wait_ge(mean_done, 1)
                for f in range(FC):
                    m = g.tensor_tensor(w2_full[:, f, :], w2_full[:, f, :], mean_row, ALU.subtract)
                m.then_inc(w2_centred, 1)

            def step(i, j):
                early = isinstance(i, int) and i < 3
                if here(i - 4) and here(i - 1):
                    rs_ln2(i - 4)
                if here(i - 3):
                    for stage in range(3):
                        fold(i - 3, stage)
                if here(i + 1):
                    keeps(i + 1, (j + 1) % JT, 0, KEEPS)
                if here(i - 3) and here(i - 1):
                    lo_u(i - 3)
                if here(i - 4) and not here(i - 1):
                    rs_ln2(i - 4)
                if here(i - 1) and not early:
                    rs_ln1(i - 1)
                if early:
                    keeps(i + 1, (j + 1) % JT, KEEPS, 6)
                if here(i):
                    beta_arg(i, 0)
                    beta_arg(i, 1)
                if here(i):
                    gamma_arg(i, 0)
                    gamma_arg(i, 1)
                if here(i - 1) and early:
                    rs_ln1(i - 1)
                if isinstance(i, int) and i == 0:
                    ternary_w2()
                if isinstance(i, int) and i == 2:
                    centre_w2()
                    g.wait_ge(const_done, 1)
                    add_const(0, 0)
                if here(i + 1) and not early:
                    keeps(i + 1, (j + 1) % JT, KEEPS, 6)
                if here(i - 4):
                    rs_ln3(i - 4)
                if here(i - 1) and not (isinstance(i, int) and i == 1):
                    add_const(i - 1, (j - 1) % JT)

            keeps(0, 0, 0, 6)
            steps(step, g)


_INS = ["hidden", "Wk", "Wv", "Wr", "Wo", "time_decay", "time_first", "time_mix_key", "time_mix_value",
        "time_mix_receptance"]
_FFN = ["ln1_g", "ln1_b", "w1", "b1", "ln2_g", "ln2_b", "w2", "b2"]


def kernel(**inputs):
    import concourse.bacc as bacc
    from concourse.bass_utils import run_bass_kernel_spmd

    nc = bacc.Bacc("TRN2", target_bir_lowering=False, num_devices=1)
    names = [f"L0_attn_{n}" for n in _INS] + [f"L0_ffn_{n}" for n in _FFN]
    laid = {name: inputs[name] for name in names}
    for name in laid:
        a = np.asarray(laid[name])
        if name.endswith(("_w1", "_w2")):
            laid[name] = a.T
        elif a.ndim == 1 and not name.endswith("_b2"):
            laid[name] = a.reshape(-1, P).T
    hidden = laid.pop("L0_attn_hidden")
    laid = {"hidden": hidden, "hidden_by_channel": np.transpose(np.asarray(hidden), (0, 2, 1)), **laid}
    arrays, args = {}, []
    for name, a in laid.items():
        a = np.ascontiguousarray(a)
        arrays[f"in_{name}"] = a
        args.append(nc.dram_tensor(f"in_{name}", a.shape, mybir.dt.from_np(a.dtype), kind="ExternalInput").ap())
    shape = inputs["L0_attn_hidden"].shape
    args.append(nc.dram_tensor("out", shape, F32, kind="ExternalOutput").ap())
    build(nc, *args)
    return run_bass_kernel_spmd(nc, [arrays], core_ids=[0]).results[0]["out"]
```
